# Optimizing a Trainium2 kernel written in Bass

```python
import numpy as np
import jax
import jax.numpy as jnp

def _softmax(x, axis=-1):
    return jax.nn.softmax(x, axis=axis)

def _gelu(x):
    return jax.nn.gelu(x, approximate=True)

def _silu(x):
    return jax.nn.silu(x)

def _sigmoid(x):
    return jax.nn.sigmoid(x)

def _layernorm(x, axis=-1, eps=1e-05):
    m = jnp.mean(x, axis=axis, keepdims=True)
    v = jnp.var(x, axis=axis, keepdims=True)
    return (x - m) / jnp.sqrt(v + eps)

def _scatter_add(tgt, idx, src, axis=0):
    return tgt.at[idx].add(src)

def _segment_sum(src, seg, n):
    return jax.ops.segment_sum(src, seg, n)
kernel_name = 'mk_gnn_preln_d2_gnn_r64_a2e471'

def setup_inputs(seed: int=0):
    np.random.seed(seed)
    _w = jnp.asarray

    def _rec_inputs():
        import jax
        import jax.numpy as jnp
        _gk = jax.random.key(seed)
        x = -0.0003713 + 1 * jax.random.normal(jax.random.fold_in(_gk, 1), (100000, 128), jnp.float32)
        src = jax.random.randint(jax.random.fold_in(_gk, 2), (50000,), 0, 100000, jnp.int32)
        dst = jax.random.randint(jax.random.fold_in(_gk, 3), (50000,), 0, 100000, jnp.int32)
        _o = jnp.argsort(dst, stable=True)
        src = src[_o]
        dst = dst[_o]
        edge_attr_20 = jax.random.uniform(jax.random.fold_in(_gk, 12), (50000, 20), jnp.float32, 0.0, 1)
        edge_weight = jax.random.uniform(jax.random.fold_in(_gk, 13), (50000,), jnp.float32, 0.0, 0.999998)
        return (x, src, dst, edge_attr_20, edge_weight)
    x, src, dst, edge_attr_20, edge_weight = _rec_inputs()

    def _L0_gnn_setup():
        import jax, jax.numpy as jnp
        import numpy as np
        N_NODES = 100000
        N_EDGES = 25000
        IN_DIM = 128
        HEADS = 4
        OUT_C = 32
        NEG_SLOPE = 0.2
        key = jax.random.key(seed)
        ks = jax.random.split(key, 8)
        x = jax.random.normal(ks[0], (N_NODES, IN_DIM), dtype=jnp.float32)
        s = float(np.sqrt(2.0 / (IN_DIM + HEADS * OUT_C)))
        W_l = jax.random.normal(ks[1], (IN_DIM, HEADS * OUT_C), dtype=jnp.float32) * s
        b_l = jnp.zeros((HEADS * OUT_C,), dtype=jnp.float32)
        W_r = jax.random.normal(ks[2], (IN_DIM, HEADS * OUT_C), dtype=jnp.float32) * s
        b_r = jnp.zeros((HEADS * OUT_C,), dtype=jnp.float32)
        att = jax.random.normal(ks[3], (HEADS, OUT_C), dtype=jnp.float32) * float(np.sqrt(2.0 / (HEADS + OUT_C)))
        bias = jnp.zeros((HEADS * OUT_C,), dtype=jnp.float32)
        src = jax.random.randint(ks[4], (N_EDGES,), 0, N_NODES, dtype=jnp.int64)
        dst = jax.random.randint(ks[5], (N_EDGES,), 0, N_NODES, dtype=jnp.int64)
        dst = jnp.where(dst == src, (dst + 1) % N_NODES, dst)
        return {'x': x, 'W_l': W_l, 'b_l': b_l, 'W_r': W_r, 'b_r': b_r, 'att': att, 'bias': bias, 'src': src, 'dst': dst}
    _L0_gnn_all = _L0_gnn_setup()
    _L0_gnn_in = {k: v for k, v in _L0_gnn_all.items() if k in ('W_l', 'b_l', 'W_r', 'b_r', 'att', 'bias')}
    del _L0_gnn_all

    def _L1_gnn_setup():
        import jax, jax.numpy as jnp
        import numpy as np
        LOG2 = float(np.log(2.0))

        def shifted_softplus(x):
            return jax.nn.softplus(x) - LOG2
        key = jax.random.key(seed)
        ks = jax.random.split(key, 12)
        n_atoms, n_edges = (20000, 10000)
        n_atom_basis, n_rbf, n_filters = (128, 20, 128)
        s = lambda fan_in: 1.0 / np.sqrt(fan_in)
        return {'x': jax.random.normal(ks[0], (n_atoms, n_atom_basis), jnp.float32), 'f_ij': jax.random.uniform(ks[1], (n_edges, n_rbf), jnp.float32), 'rcut_ij': jax.random.uniform(ks[2], (n_edges,), jnp.float32), 'idx_i': jnp.sort(jax.random.randint(ks[3], (n_edges,), 0, n_atoms)), 'idx_j': jax.random.randint(ks[4], (n_edges,), 0, n_atoms), 'W_in2f': jax.random.normal(ks[5], (n_atom_basis, n_filters), jnp.float32) * s(n_atom_basis), 'Wf1': jax.random.normal(ks[6], (n_rbf, n_filters), jnp.float32) * s(n_rbf), 'bf1': jnp.zeros((n_filters,), jnp.float32), 'Wf2': jax.random.normal(ks[7], (n_filters, n_filters), jnp.float32) * s(n_filters), 'bf2': jnp.zeros((n_filters,), jnp.float32), 'Wo1': jax.random.normal(ks[8], (n_filters, n_atom_basis), jnp.float32) * s(n_filters), 'bo1': jnp.zeros((n_atom_basis,), jnp.float32), 'Wo2': jax.random.normal(ks[9], (n_atom_basis, n_atom_basis), jnp.float32) * s(n_atom_basis), 'bo2': jnp.zeros((n_atom_basis,), jnp.float32)}
    _L1_gnn_all = _L1_gnn_setup()
    _L1_gnn_in = {k: v for k, v in _L1_gnn_all.items() if k in ('W_in2f', 'Wf1', 'bf1', 'Wf2', 'bf2', 'Wo1', 'bo1', 'Wo2', 'bo2')}
    del _L1_gnn_all
    return {'x': x, 'src': src, 'dst': dst, 'edge_attr_20': edge_attr_20, 'edge_weight': edge_weight, 'L0_gnn_W_l': _L0_gnn_in['W_l'], 'L0_gnn_b_l': _L0_gnn_in['b_l'], 'L0_gnn_W_r': _L0_gnn_in['W_r'], 'L0_gnn_b_r': _L0_gnn_in['b_r'], 'L0_gnn_att': _L0_gnn_in['att'], 'L0_gnn_bias': _L0_gnn_in['bias'], 'L1_gnn_W_in2f': _L1_gnn_in['W_in2f'], 'L1_gnn_Wf1': _L1_gnn_in['Wf1'], 'L1_gnn_bf1': _L1_gnn_in['bf1'], 'L1_gnn_Wf2': _L1_gnn_in['Wf2'], 'L1_gnn_bf2': _L1_gnn_in['bf2'], 'L1_gnn_Wo1': _L1_gnn_in['Wo1'], 'L1_gnn_bo1': _L1_gnn_in['bo1'], 'L1_gnn_Wo2': _L1_gnn_in['Wo2'], 'L1_gnn_bo2': _L1_gnn_in['bo2']}

def reference(x, src, dst, edge_attr_20, edge_weight, L0_gnn_W_l, L0_gnn_b_l, L0_gnn_W_r, L0_gnn_b_r, L0_gnn_att, L0_gnn_bias, L1_gnn_W_in2f, L1_gnn_Wf1, L1_gnn_bf1, L1_gnn_Wf2, L1_gnn_bf2, L1_gnn_Wo1, L1_gnn_bo1, L1_gnn_Wo2, L1_gnn_bo2):
    import jax
    import jax.numpy as jnp

    def _L0_gnn_ref(x, W_l, b_l, W_r, b_r, att, bias, src, dst):
        import jax, jax.numpy as jnp
        import numpy as np
        N_NODES = 100000
        N_EDGES = 25000
        IN_DIM = 128
        HEADS = 4
        OUT_C = 32
        NEG_SLOPE = 0.2
        N = x.shape[0]
        H, C = att.shape
        x_l = (x @ W_l + b_l).reshape(N, H, C)
        x_r = (x @ W_r + b_r).reshape(N, H, C)
        loop = jnp.arange(N, dtype=src.dtype)
        s = jnp.concatenate([src, loop])
        d = jnp.concatenate([dst, loop])
        m = x_l[s] + x_r[d]
        m = jnp.where(m >= 0, m, NEG_SLOPE * m)
        e = jnp.einsum('ehc,hc->eh', m, att)
        seg_max = jax.ops.segment_max(e, d, num_segments=N)
        e = jnp.exp(e - seg_max[d])
        denom = jax.ops.segment_sum(e, d, num_segments=N)
        alpha = e / denom[d]
        out = jax.ops.segment_sum(alpha[:, :, None] * x_l[s], d, num_segments=N)
        return out.reshape(N, H * C) + bias

    def _L1_gnn_ref(x, f_ij, rcut_ij, idx_i, idx_j, W_in2f, Wf1, bf1, Wf2, bf2, Wo1, bo1, Wo2, bo2):
        import jax, jax.numpy as jnp
        import numpy as np
        LOG2 = float(np.log(2.0))

        def shifted_softplus(x):
            return jax.nn.softplus(x) - LOG2
        n_atoms = x.shape[0]
        h = x @ W_in2f
        Wij = shifted_softplus(f_ij @ Wf1 + bf1) @ Wf2 + bf2
        Wij = Wij * rcut_ij[:, None]
        msg = h[idx_j] * Wij
        agg = jax.ops.segment_sum(msg, idx_i, num_segments=n_atoms)
        out = shifted_softplus(agg @ Wo1 + bo1) @ Wo2 + bo2
        return out
    h = jnp.maximum(_layernorm(x, axis=-1), 0.0)
    x = x + _L0_gnn_ref(h, L0_gnn_W_l, L0_gnn_b_l, L0_gnn_W_r, L0_gnn_b_r, L0_gnn_att, L0_gnn_bias, src, dst)
    h = jnp.maximum(_layernorm(x, axis=-1), 0.0)
    x = x + _L1_gnn_ref(h, edge_attr_20, edge_weight, src, dst, L1_gnn_W_in2f, L1_gnn_Wf1, L1_gnn_bf1, L1_gnn_Wf2, L1_gnn_bf2, L1_gnn_Wo1, L1_gnn_bo1, L1_gnn_Wo2, L1_gnn_bo2)
    return x

_drawn_inputs = setup_inputs


def setup_inputs(seed=0):
    import zlib

    import numpy as np

    out = dict(_drawn_inputs(seed))
    spreads = {'L0_gnn_b_l': (0.0, 0.1),
     'L0_gnn_b_r': (0.0, 0.8),
     'L0_gnn_bias': (0.0, 0.1),
     'L1_gnn_bf1': (0.0, 0.8),
     'L1_gnn_bf2': (0.0, 0.62),
     'L1_gnn_bo1': (0.0, 0.1),
     'L1_gnn_bo2': (0.0, 0.1)}
    factors = {'edge_attr_20': 3.116, 'edge_weight': 2.974}
    for name, (base, spread) in spreads.items():
        noise = np.random.default_rng([zlib.crc32(name.encode()), seed]).standard_normal(out[name].shape)
        drawn = base * np.exp(spread * noise) if base else spread * noise
        out[name] = jnp.asarray(drawn.astype(out[name].dtype))
    for name, factor in factors.items():
        out[name] = (out[name] * factor).astype(out[name].dtype)
    return out
```

```python
from contextlib import ExitStack

import concourse.bass as bass
from concourse import mybir

P = 128
F = 128
HEADS = 4
HC = F // HEADS
TILES = 4
C = TILES * P
J = 16
GROUP = J * P
QUADS = J // 4
RING_D = 3
EPS = 1e-5
SLOPE = 0.2
SKIP = 1 << 20

ALU = mybir.AluOpType
ACT = mybir.ActivationFunctionType
F32 = mybir.dt.float32
BF16 = mybir.dt.bfloat16
I32 = mybir.dt.int32


def turn(k, u):
    return k + u // 2 + 1


def gnn(nc, x, src, dst, edge_attr, edge_weight, W_l, b_l, W_r, b_r, att, bias,
        W_in, Wf1, bf1, Wf2, bf2, Wo1, bo1, Wo2, bo2, out):
    N = x.shape[0]
    E = src.shape[0]
    RBF = edge_attr.shape[1]
    NC = -(-E // C)
    NC += NC % 2
    NG = -(-N // GROUP)
    FULL = E // C
    REST = E - FULL * C
    assert NG == NC // 2
    assert REST and NC == FULL + 1 and NC <= P and NC >= 6 and NG >= 4

    x1_dram = nc.dram_tensor("x1_dram", (N, F), F32).ap()
    x1_end_dram = nc.dram_tensor("x1_end_dram", (NC, P, TILES * F), F32).ap()
    sum_dram = nc.dram_tensor("sum_dram", (N + C, F), F32).ap()
    goes_dram = nc.dram_tensor("goes_dram", (NC, C), BF16).ap()
    src_dram = nc.dram_tensor("src_dram", (NC, C), F32).ap()
    keep_dram = nc.dram_tensor("keep_dram", (NC, C), BF16).ap()
    weight_dram = nc.dram_tensor("weight_dram", (NC, C), F32).ap()
    attr_dram = nc.dram_tensor("attr_dram", (NC * C, RBF), F32).ap()

    with ExitStack() as ctx:
        def sb(name, shape, dt=F32):
            return ctx.enter_context(nc.sbuf_tensor(name, shape, dt))

        def two(name, shape, dt=F32):
            return [sb(f"{name}{i}", shape, dt) for i in range(2)]

        def sem(name):
            return ctx.enter_context(nc.semaphore(name))

        def sems(name, n=2):
            return [sem(f"{name}{i}") for i in range(n)]

        bank = [ctx.enter_context(nc.psum_tensor(f"bank{i}", [P, 512], F32)) for i in range(8)]

        wl = sb("wl", [P, F]); neg_wl = sb("neg_wl", [P, F]); wr = sb("wr", [P, F]); wlr = sb("wlr", [P, F])
        win = sb("win", [P, F]); wf1 = sb("wf1", [32, F]); wf2 = sb("wf2", [P, F])
        wo1 = sb("wo1", [P, F]); wo2 = sb("wo2", [P, F])
        ident = sb("ident", [P, P])
        heads = sb("heads", [P, F])
        att_relu = sb("att_relu", [P, F])
        neg_att_relu = sb("neg_att_relu", [P, F])
        att_lin = sb("att_lin", [P, F])
        cols = sb("cols", [P, 8])
        rows3 = sb("rows3", [3, 4 * F])
        part3 = sb("part3", [3, 3, 3 * F])
        part3b = sb("part3b", [3, 2, 3 * F], BF16)
        sel3 = sb("sel3", [3, 2, 3 * F])
        bias3 = sb("bias3", [3, 4, F], BF16)
        bo23 = sb("bo23", [3, 4, F], BF16)
        bo13 = sb("bo13", [3, F], BF16)
        ones3 = sb("ones3", [3, 512], BF16)
        index = sb("index", [P, 12 * NC], I32)
        columns = sb("columns", [P, 8 * NC])
        dump = sb("dump", [P, TILES])
        dump_i = sb("dump_i", [P, TILES], I32)
        lower = sb("lower", [P, TILES * P])
        clear_rows = N + C - (NG - 1) * GROUP
        zero = sb("zero", [P, clear_rows])

        def ring(name):
            return [sb(f"{name}{i}", [P, J * F]) for i in range(RING_D)]

        d_x = ring("d_x")
        d_n = ring("d_n")
        d_x1 = ring("d_x1")
        turned = [sb(f"turned{i}", [P, 512]) for i in range(2)]

        with ExitStack() as place:
            def at(name, shape, dt=F32):
                return place.enter_context(nc.sbuf_tensor(name, shape, dt))

            raw = at("raw", [P, 4, C], I32)
            rawf = at("rawf", [P, 4, C])
            goes_f = at("goes_f", [P, C])
            goes_b = at("goes_b", [P, C], BF16)
            keep_b = at("keep_b", [P, C], BF16)
            gather_f = at("gather_f", [P, C])
            scatter_f = at("scatter_f", [P, C])
            weight_f = at("weight_f", [P, C])
        with ExitStack() as place:
            def at2(name, shape, dt=F32):
                return [at(f"{name}{i}", shape, dt) for i in range(2)]

            b_x = at2("b_x", [P, TILES * F])
            b_fa = at2("b_fa", [P, TILES * RBF])
            b_goes = at2("b_goes", [P, C], BF16)
            b_w = at2("b_w", [P, C])
            b_src = at2("b_src", [P, C])
            b_n = at("b_n", [P, TILES * F])
            b_h = at("b_h", [P, C])
            b_f = at("b_f", [32, C])
            b_abs = at("b_abs", [P, C])
            b_exp = at("b_exp", [P, C])
            b_ln = at("b_ln", [P, C])
            b_s1 = at("b_s1", [P, C])
            b_neg = at("b_neg", [P, C])
            b_fill = at2("b_fill", [P, C])
            b_t = at("b_t", [P, C])
            b_msg = at("b_msg", [P, C])
            b_rows = at("b_rows", [P, TILES * F])
            b_same = at("b_same", [P, TILES, C])
            b_before = at("b_before", [P, TILES * P])
            b_sum = at2("b_sum", [P, TILES * F])
            b_dup = at("b_dup", [P, TILES])
            b_at = at2("b_at", [P, TILES], I32)
            b_col = at2("b_col", [P, 2 * TILES])
        a_xs = two("a_xs", [P, TILES * F])
        a_xd = two("a_xd", [P, TILES * F])
        a_ns = sb("a_ns", [P, TILES * F])
        a_nd = sb("a_nd", [P, TILES * F])
        a_hs = sb("a_hs", [P, C])
        a_hd = sb("a_hd", [P, C])
        a_us = sb("a_us", [P, C])
        a_u = sb("a_u", [P, C])
        a_v = two("a_v", [P, C])
        a_keep = two("a_keep", [P, C], BF16)
        a_max = two("a_max", [P, C + 1])
        a_d1 = sb("a_d1", [P, C])
        a_d2 = sb("a_d2", [P, C])
        a_decay = sb("a_decay", [P, C])
        a_p = sb("a_p", [P, C])
        a_ps = sb("a_ps", [P, C])
        a_dec = sb("a_dec", [P, C])
        a_pv = sb("a_pv", [P, C])
        a_den = two("a_den", [P, C])
        a_sum = two("a_sum", [P, C])
        a_all = sb("a_all", [P, C])
        a_log = sb("a_log", [P, C])
        a_rec = sb("a_rec", [P, C])
        a_o = two("a_o", [P, C])
        a_base = two("a_base", [P, TILES * F])
        a_x1 = two("a_x1", [P, TILES * F])
        ones = sb("ones", [P, 1])
        f_abs_out = sb("f_abs_out", [P, 512]); f_exp_out = sb("f_exp_out", [P, 512])
        f_ln_out = two("f_ln_out", [P, 512]); f_ssp_out = two("f_ssp_out", [P, 512])

        def stat(name, n, rings):
            return [{"six": sb(f"{name}_six{i}", [P, n, 6]),
                     "sum": sb(f"{name}_sum{i}", [P, n]),
                     "dif": sb(f"{name}_dif{i}", [P, n]),
                     "sq": sb(f"{name}_sq{i}", [P, n]),
                     "sq2": sb(f"{name}_sq2{i}", [P, n]),
                     "var": sb(f"{name}_var{i}", [P, n]),
                     "log": sb(f"{name}_log{i}", [P, n]),
                     "rstd": sb(f"{name}_rstd{i}", [P, n]),
                     "shift": sb(f"{name}_shift{i}", [P, n])}
                    for i in range(rings)]

        stat_d = stat("stat_d", J, 2)
        stat_e = stat("stat_e", 2 * TILES, 2)

        gidx = [sb(f"gidx{i}", [P, 8], I32) for i in range(2)]
        sidx = [sb(f"sidx{i}", [P, 4], I32) for i in range(2)]

        load_const = sem("load_const"); pool_zero = sem("pool_zero"); pool_const = sem("pool_const")
        pads_set = sem("pads_set"); load_raw = sem("load_raw"); load_weight = sem("load_weight")
        pool_step = sem("pool_step"); sync_step = sem("sync_step")
        setup = sem("setup")
        weights_ready = sem("weights_ready"); columns_ready = sem("columns_ready"); zero_set = sem("zero_set")
        keep_ready = sem("keep_ready"); index_f_ready = sem("index_f_ready"); index_turned = sem("index_turned")
        index_ready = sem("index_ready"); store_setup = sem("store_setup"); parts = sem("parts")

        xd_loaded = sems("xd_loaded", RING_D); x1_stored = sems("x1_stored", RING_D)
        d_six = sem("d_six"); d_sumdif = sem("d_sumdif"); d_sq = sem("d_sq"); d_var = sem("d_var")
        d_log = sem("d_log"); d_rstd = sem("d_rstd"); d_shift = sem("d_shift")
        d_norm_act = sem("d_norm_act"); d_norm_dve = sem("d_norm_dve")
        d_turned = sem("d_turned"); d_relu = sem("d_relu"); d_mm = sem("d_mm"); d_x1_ready = sem("d_x1_ready")

        gidx_loaded = sems("gidx_loaded"); keep_loaded = sems("keep_loaded")
        src_gathered = sems("src_gathered"); dst_gathered = sems("dst_gathered")
        cleared = sem("cleared"); end_stored = sems("end_stored")
        six = sem("six"); sumdif = sem("sumdif"); sq = sem("sq"); var = sem("var")
        log_var = sem("log_var"); rstd = sem("rstd"); shift = sem("shift")
        norm_src = sem("norm_src"); norm_dst = sem("norm_dst")
        turned_src = sem("turned_src"); turned_dst = sem("turned_dst")
        h_src = sem("h_src"); h_dst = sem("h_dst")
        self_mm = sem("self_mm"); v_mm = sem("v_mm"); edge_mm = sem("edge_mm"); base_mm = sem("base_mm")
        self_relu = sem("self_relu"); v_copied = sem("v_copied"); edge_relu = sem("edge_relu")
        score_mm = sem("score_mm"); max_carry = sem("max_carry"); max_scan = sem("max_scan")
        dif_decay = sem("dif_decay"); dif_score = sem("dif_score")
        exp_decay = sem("exp_decay"); exp_score = sem("exp_score"); exp_self = sem("exp_self")
        decay = sem("decay"); weighted = sem("weighted"); den_scan = sem("den_scan"); sum_scan = sem("sum_scan")
        den_all = sem("den_all"); den_log = sem("den_log"); den_rec = sem("den_rec")
        base_ready = sem("base_ready"); att_out = sem("att_out"); out_turned = sem("out_turned")
        x1_ready = sem("x1_ready")

        b_x_ld = sems("b_x_ld"); b_fa_ld = sems("b_fa_ld"); b_goes_ld = sems("b_goes_ld"); b_w_ld = sems("b_w_ld")
        b_src_ld = sems("b_src_ld"); b_sidx_ld = sems("b_sidx_ld"); b_col_ld = sems("b_col_ld")
        x1_scattered = sems("x1_scattered"); added = sems("added")
        ones_set = sem("ones_set"); b_six = sem("b_six"); b_sumdif = sem("b_sumdif"); b_sq = sem("b_sq")
        b_var = sem("b_var"); b_logv = sem("b_logv"); b_rstd = sem("b_rstd"); b_shift = sem("b_shift")
        b_norm = sem("b_norm")
        b_fa_turned = sem("b_fa_turned"); b_f_ready = sem("b_f_ready"); b_z1 = sem("b_z1")
        b_abs_done = sem("b_abs_done"); b_exp_done = sem("b_exp_done"); b_ln_done = sem("b_ln_done")
        b_s1_ready = sem("b_s1_ready"); b_turned = sem("b_turned"); b_h_ready = sem("b_h_ready")
        b_hf = sem("b_hf"); b_filter = sem("b_filter"); b_neg_ready = sem("b_neg_ready")
        b_fill_ready = sem("b_fill_ready"); b_t_ready = sem("b_t_ready"); b_msg_ready = sem("b_msg_ready")
        b_msg_turned = sem("b_msg_turned"); b_rows_ready = sem("b_rows_ready"); b_same_ready = sem("b_same_ready")
        b_before_ready = sem("b_before_ready"); b_count = sem("b_count"); b_dup_ready = sem("b_dup_ready")
        b_at_ready = sem("b_at_ready"); b_summed = sem("b_summed"); b_sum_ready = sem("b_sum_ready")

        f_x1_ld = sems("f_x1_ld", RING_D); f_sum_ld = sems("f_sum_ld", RING_D); out_stored = sems("out_stored", RING_D)
        f_turned = sem("f_turned"); f_copied = sem("f_copied"); f_z = sem("f_z"); f_abs = sem("f_abs")
        f_exp = sem("f_exp"); f_ln = sem("f_ln"); f_s = sem("f_s"); f_y = sem("f_y"); f_out = sem("f_out")

        N_CONST = 16
        N_RAW = 9
        slots3 = [len(range(i, NG, RING_D)) for i in range(RING_D)]
        HALF = NC // 2
        bound = N - 1

        def node_rows(a, g):
            start = g * GROUP if not isinstance(g, int) or g < NG - 1 else N - GROUP
            return a[bass.ds(start, GROUP), :].rearrange("(p j) f -> p (j f)", p=P)

        block = ctx.enter_context(nc.Block())

        @block.sync
        def _(sp):
            def const(tile, a):
                sp.dma_start(tile, a).then_inc(load_const, 16)

            for tile, a in ((wl, W_l), (wr, W_r), (win, W_in), (wf2, Wf2), (wo1, Wo1), (wo2, Wo2)):
                const(tile[:, :], a)
            const(wf1[0:RBF, :], Wf1)
            const(wf1[RBF:RBF + 1, :], bf1.rearrange("(a f) -> a f", a=1))
            const(cols[:, 0:1], att.rearrange("h (c o) -> (h c) o", o=1))
            for n, a in enumerate((b_l, b_r)):
                const(cols[:, 1 + n:2 + n], a.rearrange("(f o) -> f o", o=1))
            const(cols[:, 4:5], bf2.rearrange("(f o) -> f o", o=1))
            for n, a in enumerate((b_l, bias, bo2, bo1)):
                const(rows3[:, n * F:(n + 1) * F], a.rearrange("(a f) -> a f", a=1).broadcast_to([3, F]))
            sp.wait_ge(pads_set, 1)

            def by_chunk(i, r0, r1, a):
                sp.dma_start(raw[r0:r1, i, :], a.rearrange("(r c) -> r c", c=C)).then_inc(load_raw, 16)

            def part(i, r, c0, a):
                sp.dma_start(raw[r:r + 1, i, c0:c0 + a.shape[0]], a.rearrange("(o c) -> o c", o=1)).then_inc(load_raw, 16)

            by_chunk(0, 0, FULL, src[0:FULL * C])
            part(0, FULL, 0, src[FULL * C:E])
            by_chunk(1, 0, FULL, dst[0:FULL * C])
            part(1, FULL, 0, dst[FULL * C:E])
            by_chunk(2, 0, FULL, dst[1:FULL * C + 1])
            part(2, FULL, 0, dst[FULL * C + 1:E])
            part(3, 0, 1, dst[0:C - 1])
            by_chunk(3, 1, FULL, dst[C - 1:FULL * C - 1])
            part(3, FULL, 0, dst[FULL * C - 1:E - 1])
            sp.dma_start(weight_f[0:FULL, :], edge_weight[0:FULL * C].rearrange("(r c) -> r c", c=C)).then_inc(load_weight, 16)
            sp.dma_start(weight_f[FULL:NC, 0:REST], edge_weight[FULL * C:E].rearrange("(r c) -> r c", r=1)).then_inc(load_weight, 16)
            sp.dma_start(d_x[0][:, :], node_rows(x, 0)).then_inc(xd_loaded[0], 16)
            sp.dma_start(d_x[1][:, :], node_rows(x, 1)).then_inc(xd_loaded[1], 16)
            sp.dma_start(d_x[2][:, :], node_rows(x, 2)).then_inc(xd_loaded[2], 16)
            sp.wait_ge(zero_set, 1)
            flat = attr_dram.rearrange("e r -> (e r)")
            sp.dma_start(flat[0:E * RBF].rearrange("(a b) -> a b", a=400),
                         edge_attr.rearrange("e r -> (e r)").rearrange("(a b) -> a b", a=400)).then_inc(store_setup, 16)
            pad_rows = (NC * C - E) * RBF // 32
            sp.dma_start(flat[E * RBF:NC * C * RBF].rearrange("(a b) -> a b", b=32), zero[0:pad_rows, 0:32]).then_inc(store_setup, 16)
            sp.wait_ge(load_weight, 32)
            sp.dma_start(weight_dram, weight_f[0:NC, :]).then_inc(store_setup, 16)
            sp.wait_ge(keep_ready, 3)
            sp.dma_start(keep_dram, keep_b[0:NC, :]).then_inc(store_setup, 16)
            sp.dma_start(goes_dram, goes_b[0:NC, :]).then_inc(store_setup, 16)
            sp.dma_start(src_dram, rawf[0:NC, 0, :]).then_inc(store_setup, 16)

            def stores(g, slot, turn3):
                sp.wait_ge(d_x1_ready, QUADS * g + QUADS)
                sp.dma_start(node_rows(x1_dram, g), d_x1[slot][:, :]).then_inc(x1_stored[slot], 16)

            def load(g, slot):
                sp.dma_start(d_x[slot][:, :], node_rows(x, g)).then_inc(xd_loaded[slot], 16)

            TRIPLES = (NG - 1 - RING_D) // RING_D
            with sp.Fori(0, TRIPLES) as m:
                for i in range(RING_D):
                    g = m * RING_D + i
                    stores(g, i, m)
                    load(g + RING_D, i)
            for g in range(TRIPLES * RING_D, NG):
                if g == NG - 1:
                    sp.wait_ge(x1_stored[(g - 1) % RING_D], 16 * slots3[(g - 1) % RING_D])
                stores(g, g % RING_D, g // RING_D)
                if g + RING_D < NG:
                    load(g + RING_D, g % RING_D)

            sp.wait_ge(store_setup, 96)
            sp.wait_ge(index_ready, 3)
            sum_flat = sum_dram.rearrange("n f -> (n f)")

            def clear(k):
                if isinstance(k, int) and k == NG - 1:
                    sp.dma_start(sum_flat[k * GROUP * F:(N + C) * F].rearrange("(p m) -> p m", p=P), zero[:, :]).then_inc(cleared, 16)
                else:
                    sp.dma_start(sum_flat[bass.ds(k * GROUP * F, GROUP * F)].rearrange("(p m) -> p m", p=P),
                                 zero[:, 0:J * F]).then_inc(cleared, 16)

            def load_gidx(k, u):
                s = u % 2
                sp.dma_start(gidx[s][:, :], index[:, bass.ds(12 * (2 * k + u), 8)]).then_inc(gidx_loaded[s], 16)

            def step_a(k, u, t0, gather=True, keep=True, end=True):
                s = u % 2
                if gather:
                    sp.wait_ge(src_gathered[s], 64 * turn(k, u))
                    sp.wait_ge(dst_gathered[s], 64 * turn(k, u))
                    load_gidx(k, u + 2)
                if keep:
                    if t0 >= 2:
                        sp.wait_ge(sum_scan, 2 * k + u - 1)
                    sp.dma_start(a_keep[s][:, :], keep_dram[bass.ds(2 * k + u, 1), :].broadcast_to([P, C])).then_inc(keep_loaded[s], 16)
                if end and t0 >= 3:
                    sp.wait_ge(x1_ready, 2 * k + u - 2)
                    sp.dma_start(x1_end_dram[bass.ds(2 * k + u - 3, 1), :, :].rearrange("o p f -> (o p) f"),
                                 a_x1[1 - s][:, :]).then_inc(end_stored[1 - s], 16)

            load_gidx(0, 0)
            load_gidx(0, 1)
            for u in range(4):
                step_a(0, u, u)
                if u % 2:
                    clear(u // 2)
            with sp.Fori(2, HALF - 1) as k:
                for u in range(2):
                    step_a(k, u, 4 + u)
                clear(k)
            for u in range(5):
                step_a(HALF - 1, u, 4 + u, gather=False, keep=u < 2)
            clear(HALF - 1)

            for s in range(2):
                sp.wait_ge(end_stored[s], 16 * HALF)
            sp.wait_ge(columns_ready, 1)

            def step_b(k, u, t0):
                s = u % 2
                t = 2 * k + u
                if t0 >= 2:
                    sp.wait_ge(b_fa_turned, t - 1)
                    sp.sem_inc(sync_step, 1)
                sp.dma_start(b_fa[s][:, :], attr_dram[bass.ds((NC - 1 - t) * C, C), :].rearrange("(p j) r -> p (j r)", p=P)).then_inc(b_fa_ld[s], 16)
                if t0 >= 2:
                    sp.wait_ge(x1_scattered[s], 64 * turn(k, u - 2))
                    sp.wait_ge(b_norm, t - 1)
                    sp.sem_inc(sync_step, 1)
                sp.dma_start(b_x[s][:, :], x1_end_dram[bass.ds(NC - 1 - t, 1), :, :].rearrange("o p f -> (o p) f")).then_inc(b_x_ld[s], 16)
                sp.dma_start(sidx[s][:, :], index[:, bass.ds(12 * (NC - 1 - t) + 8, 4)]).then_inc(b_sidx_ld[s], 16)
                if t0 >= 2:
                    sp.wait_ge(b_fill_ready, t - 1)
                    sp.sem_inc(sync_step, 1)
                sp.dma_start(b_goes[s][:, :], goes_dram[bass.ds(NC - 1 - t, 1), :].broadcast_to([P, C])).then_inc(b_goes_ld[s], 16)
                if t0 >= 2:
                    sp.wait_ge(b_at_ready, t - 1)
                    sp.sem_inc(sync_step, 1)
                sp.dma_start(b_w[s][:, :], weight_dram[bass.ds(NC - 1 - t, 1), :].broadcast_to([P, C])).then_inc(b_w_ld[s], 16)
                sp.dma_start(b_src[s][:, :], src_dram[bass.ds(NC - 1 - t, 1), :].broadcast_to([P, C])).then_inc(b_src_ld[s], 16)
                sp.dma_start(b_col[s][:, :], columns[:, bass.ds(8 * (NC - 1 - t), 8)]).then_inc(b_col_ld[s], 16)

            for u in range(4):
                step_b(0, u, u)
            with sp.Fori(2, HALF) as k:
                for u in range(2):
                    step_b(k, u, 4 + u)

            for s in range(2):
                sp.wait_ge(x1_scattered[s], 64 * HALF)
                sp.wait_ge(added[s], 64 * HALF)

            def f_load(g, slot):
                sp.dma_start(d_n[slot][:, :], node_rows(sum_dram, g)).then_inc(f_sum_ld[slot], 16)
                sp.dma_start(d_x[slot][:, :], node_rows(x1_dram, g)).then_inc(f_x1_ld[slot], 16)

            def f_store(g, slot):
                sp.wait_ge(f_out, QUADS * g + QUADS)
                sp.dma_start(node_rows(out, g), d_x1[slot][:, :]).then_inc(out_stored[slot], 16)

            for g in range(RING_D):
                f_load(g, g)
            with sp.Fori(0, TRIPLES) as m:
                for i in range(RING_D):
                    f_store(m * RING_D + i, i)
                    f_load(m * RING_D + i + RING_D, i)
            for g in range(TRIPLES * RING_D, NG):
                if g == NG - 1:
                    sp.wait_ge(out_stored[(g - 1) % RING_D], 16 * slots3[(g - 1) % RING_D])
                f_store(g, g % RING_D)
                if g + RING_D < NG:
                    f_load(g + RING_D, g % RING_D)
            for i in range(RING_D):
                sp.wait_ge(out_stored[i], 16 * slots3[i])

        @block.gpsimd
        def _(pool):
            pool.memset(raw[:, 0, :], 0)
            pool.memset(raw[:, 1, :], SKIP)
            pool.memset(raw[:, 2:4, :], -1)
            pool.memset(weight_f[:, :], 0.0).then_inc(pads_set, 1)
            pool.memset(zero[:, :], 0.0).then_inc(zero_set, 1)
            pool.memset(lower[:, :], 0.0)
            pool.memset(ident[:, :], 0.0)
            pool.memset(ones3[:, :], 1.0).then_inc(pool_zero, 1)
            pool.wait_ge(pool_zero, 1)
            pool.affine_select(out=ident[:, :], in_=ident[:, :], compare_op=ALU.not_equal, fill=1.0, base=0,
                               pattern=[[-1, P]], channel_multiplier=1)
            pool.affine_select(out=lower[:, :].rearrange("p (j c) -> p j c", j=TILES),
                               in_=lower[:, :].rearrange("p (j c) -> p j c", j=TILES), compare_op=ALU.is_ge, fill=1.0, base=0,
                               pattern=[[0, TILES], [-1, P]], channel_multiplier=1)
            pool.iota(dump_i[:, :], pattern=[[P, TILES]], base=N, channel_multiplier=1).then_inc(pool_const, 1)

            pool.wait_ge(index_ready, 3)
            pool.wait_ge(store_setup, 96)

            def gathers(k, u, t0):
                s = u % 2
                pool.wait_ge(gidx_loaded[s], 16 * turn(k, u))
                if t0 >= 2:
                    pool.wait_ge(norm_src, 2 * k + u - 1)
                pool.sem_inc(pool_step, 1)
                for j in range(TILES):
                    pool.indirect_dma_start(a_xs[s][:, j * F:(j + 1) * F], None, x,
                                            bass.IndirectOffsetOnAxis(ap=gidx[s][:, j:j + 1], axis=0)).then_inc(src_gathered[s], 16)
                if t0 >= 2:
                    pool.wait_ge(base_ready, 2 * k + u - 1)
                    pool.sem_inc(pool_step, 1)
                for j in range(TILES):
                    pool.indirect_dma_start(a_xd[s][:, j * F:(j + 1) * F], None, x,
                                            bass.IndirectOffsetOnAxis(ap=gidx[s][:, 4 + j:5 + j], axis=0)).then_inc(dst_gathered[s], 16)

            for u in range(4):
                gathers(0, u, u)
            with pool.Fori(2, HALF) as k:
                for u in range(2):
                    gathers(k, u, 4)

            for i in range(RING_D):
                pool.wait_ge(x1_stored[i], 16 * slots3[i])
            pool.wait_ge(cleared, 16 * NG)

            def scatters(k, u):
                s = u % 2
                pool.wait_ge(b_sidx_ld[s], 16 * turn(k, u))
                pool.wait_ge(b_x_ld[s], 16 * turn(k, u))
                pool.sem_inc(pool_step, 1)
                for j in range(TILES):
                    pool.indirect_dma_start(x1_dram, bass.IndirectOffsetOnAxis(ap=sidx[s][:, j:j + 1], axis=0),
                                            b_x[s][:, j * F:(j + 1) * F], None,
                                            bounds_check=bound, oob_is_err=False).then_inc(x1_scattered[s], 16)

            def adds(k, u, first=False):
                s = u % 2
                pool.wait_ge(b_at_ready, 2 * k + u + 1)
                pool.wait_ge(b_sum_ready, 2 * k + u + 1)
                if not first:
                    pool.wait_ge(added[1 - s], 64 * turn(k, u - 1))
                pool.sem_inc(pool_step, 1)
                for j in range(TILES):
                    pool.indirect_dma_start(sum_dram, bass.IndirectOffsetOnAxis(ap=b_at[s][:, j:j + 1], axis=0),
                                            b_sum[s][:, j * F:(j + 1) * F], None, compute_op=ALU.add).then_inc(added[s], 16)

            for u in range(4):
                scatters(0, u)
                if u >= 2:
                    adds(0, u - 2, first=u == 2)
            with pool.Fori(2, HALF) as k:
                for u in range(2):
                    scatters(k, u)
                    adds(k, u - 2)
            for u in range(2):
                adds(HALF, u - 2)

        def statistics(dve, st, n, six_done, sumdif_done, sq_done, var_done, at, count):
            dve.wait_ge(six_done, count)
            dve.tensor_tensor(st["sum"][:, 0:n], st["six"][:, 0:n, 1], st["six"][:, 0:n, 4], ALU.add)
            dve.tensor_tensor(st["sq"][:, 0:n], st["six"][:, 0:n, 2], st["six"][:, 0:n, 5], ALU.add)
            dve.tensor_tensor(st["dif"][:, 0:n], st["six"][:, 0:n, 1], st["six"][:, 0:n, 4], ALU.subtract).then_inc(sumdif_done, 1)
            dve.wait_ge(sumdif_done, count)
            dve.scalar_tensor_tensor(out=st["sq2"][:, 0:n], in0=st["dif"][:, 0:n], scalar=F / 4.0, in1=st["dif"][:, 0:n],
                                     op0=ALU.mult, op1=ALU.mult).then_inc(sq_done, 1)
            dve.wait_ge(sq_done, count)
            dve.tensor_tensor(st["var"][:, 0:n], st["sq"][:, 0:n], st["sq2"][:, 0:n], ALU.add).then_inc(var_done, 1)

        def inverse_deviation(act, st, n, var_done, log_done, rstd_done, count):
            act.wait_ge(var_done, count)
            act.activation(st["log"][:, 0:n], st["var"][:, 0:n], ACT.Ln, scale=1.0 / F, bias=EPS).then_inc(log_done, 1)
            act.wait_ge(log_done, count)
            act.activation(st["rstd"][:, 0:n], st["log"][:, 0:n], ACT.Exp, scale=-0.5).then_inc(rstd_done, 1)

        def shifts(dve, st, n, rstd_done, shift_done, count):
            dve.wait_ge(rstd_done, count)
            dve.scalar_tensor_tensor(out=st["shift"][:, 0:n], in0=st["sum"][:, 0:n], scalar=-0.5, in1=st["rstd"][:, 0:n],
                                     op0=ALU.mult, op1=ALU.mult).then_inc(shift_done, 1)

        ONE = slice(0, 1)

        @block.vector
        def _(dve):
            n_setup = [0]

            def link(ins):
                n_setup[0] += 1
                ins.then_inc(setup, 1)
                dve.wait_ge(setup, n_setup[0])

            dve.wait_ge(load_raw, 16 * N_RAW)
            dve.tensor_copy(rawf[:, :, :], raw[:, :, :]).then_inc(keep_ready, 1)
            dve.wait_ge(keep_ready, 1)
            dve.tensor_tensor(keep_b[:, :], rawf[:, 1, :], rawf[:, 3, :], ALU.is_equal).then_inc(keep_ready, 1)
            dve.tensor_scalar(gather_f[:, :], rawf[:, 1, :], float(N - 1), None, ALU.min)
            link(dve.tensor_tensor(goes_f[:, :], rawf[:, 1, :], rawf[:, 2, :], ALU.is_equal))
            dve.scalar_tensor_tensor(out=scatter_f[:, :], in0=goes_f[:, :], scalar=float(SKIP), in1=rawf[:, 1, :],
                                     op0=ALU.mult, op1=ALU.add).then_inc(index_f_ready, 1)
            dve.tensor_copy(goes_b[:, :], goes_f[:, :]).then_inc(keep_ready, 1)
            dve.memset(ones[:, :], 1.0)
            link(dve.memset(heads[:, :], 0.0))
            for h in range(HEADS):
                last = dve.memset(heads[h * HC:(h + 1) * HC, h * HC:(h + 1) * HC], 1.0)
            link(last)
            dve.wait_ge(load_const, 16 * N_CONST)
            dve.wait_ge(pool_const, 1)
            dve.tensor_scalar(neg_wl[:, :], wl[:, :], -1.0, None, ALU.mult)
            dve.tensor_tensor(wlr[:, :], wl[:, :], wr[:, :], ALU.add)
            dve.tensor_scalar(att_relu[:, :], heads[:, :], cols[:, 0:1], 1.0 - SLOPE, ALU.mult, ALU.mult)
            dve.tensor_scalar(neg_att_relu[:, :], heads[:, :], cols[:, 0:1], SLOPE - 1.0, ALU.mult, ALU.mult)
            dve.tensor_scalar(att_lin[:, :], heads[:, :], cols[:, 0:1], SLOPE, ALU.mult, ALU.mult)
            dve.tensor_tensor(cols[:, 3:4], cols[:, 1:2], cols[:, 2:3], ALU.add).then_inc(weights_ready, 1)
            dve.tensor_copy(part3[:, 0, F:3 * F], rows3[:, 2 * F:4 * F])
            link(dve.tensor_tensor(part3[:, 0, 0:F], rows3[:, 0:F], rows3[:, F:2 * F], ALU.add))
            link(dve.tensor_copy(part3b[:, 0, :], part3[:, 0, :]))
            link(dve.tensor_tensor(part3[:, 1, :], part3[:, 0, :], part3b[:, 0, :], ALU.subtract))
            link(dve.tensor_copy(part3b[:, 1, :], part3[:, 1, :]))
            link(dve.tensor_tensor(part3[:, 2, :], part3[:, 1, :], part3b[:, 1, :], ALU.subtract))
            link(dve.tensor_scalar(sel3[:, 0, :], part3b[:, 0, :], ident[0:3, 0:1], None, ALU.mult))
            link(dve.scalar_tensor_tensor(out=sel3[:, 1, :], in0=part3b[:, 1, :], scalar=ident[0:3, 1:2], in1=sel3[:, 0, :],
                                          op0=ALU.mult, op1=ALU.add))
            link(dve.scalar_tensor_tensor(out=sel3[:, 0, :], in0=part3[:, 2, :], scalar=ident[0:3, 2:3], in1=sel3[:, 1, :],
                                          op0=ALU.mult, op1=ALU.add))
            for j in range(4):
                dve.tensor_copy(bias3[:, j, :], sel3[:, 0, 0:F])
                dve.tensor_copy(bo23[:, j, :], sel3[:, 0, F:2 * F])
            dve.tensor_copy(bo13[:, :], sel3[:, 0, 2 * F:3 * F]).then_inc(parts, 1)
            dve.wait_ge(index_turned, 3)
            for i in range(3):
                dve.tensor_copy(index[:, :].rearrange("p (c i) -> p c i", i=12)[:, :, 4 * i:4 * i + 4],
                                bank[i][:, 0:4 * NC].rearrange("p (j c) -> p c j", j=4)).then_inc(index_ready, 1)
            dve.wait_ge(index_ready, 3)
            dve.tensor_copy(dump[:, :], dump_i[:, :])
            link(dve.tensor_copy(columns[:, :].rearrange("p (c i) -> p c i", i=8)[:, :, 0:4],
                                 index[:, :].rearrange("p (c i) -> p c i", i=12)[:, :, 0:4]))
            for j in range(TILES):
                last = dve.tensor_scalar(columns[:, :].rearrange("p (c i) -> p i c", i=8)[:, 4 + j, :],
                                         columns[:, :].rearrange("p (c i) -> p i c", i=8)[:, j, :],
                                         -1.0, dump[:, j:j + 1], ALU.mult, ALU.add)
            last.then_inc(columns_ready, 1)

            def step_d(g, slot, m, front=True, back=True):
                st = stat_d[0]
                if front:
                    dve.wait_ge(xd_loaded[slot], 16 * (m + 1))
                    if not (isinstance(g, int) and g == 0):
                        dve.wait_ge(d_norm_act, 3 * g)
                    for j in range(J):
                        last = dve.bn_stats(st["six"][:, j, :], d_x[slot][:, j * F:(j + 1) * F])
                    last.then_inc(d_six, 1)
                if back:
                    s1 = (slot - 1) % RING_D
                    for q in range(QUADS):
                        dve.wait_ge(d_mm, QUADS * (g - 1) + q + 1)
                        if q == 0 and not (isinstance(g, int) and g <= RING_D):
                            dve.wait_ge(x1_stored[s1], 16 * (m if slot else m - 1))
                        dve.tensor_tensor(d_x1[s1][:, q * 512:(q + 1) * 512], bank[2 + q % 2][:, :],
                                          d_x[s1][:, q * 512:(q + 1) * 512], ALU.add).then_inc(d_x1_ready, 1)
                if front:
                    statistics(dve, st, J, d_six, d_sumdif, d_sq, d_var, g, g + 1)
                    shifts(dve, st, J, d_rstd, d_shift, g + 1)
                    dve.wait_ge(d_shift, g + 1)
                    for j in range(J - 4, J):
                        last = dve.tensor_scalar(d_n[slot][:, j * F:(j + 1) * F], d_x[slot][:, j * F:(j + 1) * F],
                                                 st["rstd"][:, j:j + 1], st["shift"][:, j:j + 1], ALU.mult, ALU.add)
                    last.then_inc(d_norm_dve, 1)

            for g in range(4):
                step_d(g, g % RING_D, g // RING_D, back=g > 0)
            step_d(4, 1, 1)
            step_d(5, 2, 1)
            LOOPS = (NG - 6) // RING_D
            if LOOPS:
                with dve.Fori(2, 2 + LOOPS) as m:
                    for i in range(RING_D):
                        step_d(m * RING_D + i, i, m)
            for g in range(6 + LOOPS * RING_D, NG + 1):
                step_d(g, g % RING_D, g // RING_D, front=g < NG)

            def step_a(k, u, t0, front=True, mid=True, back=True):
                s = u % 2
                t = 2 * k + u
                st = stat_e[s]
                if front:
                    dve.wait_ge(src_gathered[s], 64 * turn(k, u))
                    for j in range(TILES):
                        dve.bn_stats(st["six"][:, j, :], a_xs[s][:, j * F:(j + 1) * F])
                    dve.wait_ge(dst_gathered[s], 64 * turn(k, u))
                    for j in range(TILES):
                        last = dve.bn_stats(st["six"][:, TILES + j, :], a_xd[s][:, j * F:(j + 1) * F])
                    last.then_inc(six, 1)
                if back:
                    dve.wait_ge(out_turned, t - 1)
                    if t0 >= 4:
                        dve.wait_ge(end_stored[s], 16 * turn(k, u - 4))
                    dve.tensor_tensor(a_x1[s][:, :], bank[7][:, :], a_base[s][:, :], ALU.add).then_inc(x1_ready, 1)
                if front:
                    statistics(dve, st, 2 * TILES, six, sumdif, sq, var, t, t + 1)
                if mid:
                    o = 1 - s
                    dve.wait_ge(score_mm, t)
                    dve.wait_ge(keep_loaded[o], 16 * turn(k, u - 1))
                    if t0 == 1:
                        dve.memset(a_max[o][:, 0:1], 0.0).then_inc(max_carry, 1)
                        first = 0.0
                    else:
                        dve.tensor_copy(a_max[o][:, 0:1], a_max[s][:, C:C + 1]).then_inc(max_carry, 1)
                        first = a_max[s][:, C:C + 1]
                    dve.tensor_tensor_scan(a_max[o][:, 1:C + 1], a_keep[o][:, :], bank[5][:, :], first,
                                           ALU.mult, ALU.max).then_inc(max_scan, 1)
                    dve.wait_ge(max_carry, t)
                    dve.wait_ge(max_scan, t)
                    dve.tensor_tensor(a_d1[:, :], a_max[o][:, 0:C], a_max[o][:, 1:C + 1], ALU.subtract).then_inc(dif_decay, 1)
                    dve.tensor_tensor(a_d2[:, :], bank[5][:, :], a_max[o][:, 1:C + 1], ALU.subtract).then_inc(dif_score, 1)
                if front:
                    shifts(dve, st, 2 * TILES, rstd, shift, t + 1)
                    dve.wait_ge(shift, t + 1)
                    for j in range(TILES):
                        last = dve.tensor_scalar(a_nd[:, j * F:(j + 1) * F], a_xd[s][:, j * F:(j + 1) * F],
                                                 st["rstd"][:, TILES + j:TILES + j + 1], st["shift"][:, TILES + j:TILES + j + 1],
                                                 ALU.mult, ALU.add)
                    last.then_inc(norm_dst, 1)
                if mid:
                    dve.wait_ge(exp_decay, t)
                    dve.scalar_tensor_tensor(out=a_dec[:, :], in0=a_decay[:, :], scalar=1.0, in1=a_keep[o][:, :],
                                             op0=ALU.min, op1=ALU.mult).then_inc(decay, 1)
                    dve.wait_ge(exp_score, t)
                    dve.tensor_tensor(a_pv[:, :], a_p[:, :], a_v[o][:, :], ALU.mult).then_inc(weighted, 1)
                    dve.wait_ge(decay, t)
                    dve.tensor_tensor_scan(a_den[o][:, :], a_dec[:, :], a_p[:, :], 0.0 if t0 == 1 else a_den[s][:, C - 1:C],
                                           ALU.mult, ALU.add).then_inc(den_scan, 1)
                    dve.wait_ge(weighted, t)
                    dve.tensor_tensor_scan(a_sum[o][:, :], a_dec[:, :], a_pv[:, :], 0.0 if t0 == 1 else a_sum[s][:, C - 1:C],
                                           ALU.mult, ALU.add).then_inc(sum_scan, 1)
                    dve.wait_ge(den_scan, t)
                    dve.wait_ge(exp_self, t)
                    dve.tensor_tensor(a_all[:, :], a_den[o][:, :], a_ps[:, :], ALU.add).then_inc(den_all, 1)
                if front:
                    dve.wait_ge(base_mm, t + 1)
                    dve.tensor_tensor(a_base[s][:, :], bank[6][:, :], a_xd[s][:, :], ALU.add).then_inc(base_ready, 1)
                if mid:
                    dve.wait_ge(den_rec, t)
                    dve.wait_ge(sum_scan, t)
                    dve.tensor_tensor(a_o[o][:, :], a_sum[o][:, :], a_rec[:, :], ALU.mult).then_inc(att_out, 1)

            for u in range(4):
                step_a(0, u, u, mid=u >= 1, back=u >= 2)
            with dve.Fori(2, HALF) as k:
                for u in range(2):
                    step_a(k, u, 4 + u)
            step_a(HALF, 0, 4, front=False)
            step_a(HALF, 1, 5, front=False, mid=False)

            for s in range(2):
                dve.wait_ge(end_stored[s], 16 * HALF)
            dve.memset(b_f[:, :], 1.0).then_inc(ones_set, 1)

            def step_b(k, u, t0, front=True, mid=True):
                s = u % 2
                o = 1 - s
                t = 2 * k + u
                st = stat_e[s]
                if front:
                    dve.wait_ge(b_x_ld[s], 16 * turn(k, u))
                    for j in range(TILES):
                        last = dve.bn_stats(st["six"][:, j, :], b_x[s][:, j * F:(j + 1) * F])
                    last.then_inc(b_six, 1)
                    statistics(dve, st, TILES, b_six, b_sumdif, b_sq, b_var, t, t + 1)
                if mid:
                    dve.wait_ge(b_hf, t)
                    dve.wait_ge(b_goes_ld[o], 16 * turn(k, u - 1))
                    dve.scalar_tensor_tensor(out=b_neg[:, :], in0=b_goes[o][:, :], scalar=1.0, in1=bank[3][:, :],
                                             op0=ALU.subtract, op1=ALU.mult).then_inc(b_neg_ready, 1)
                if front:
                    shifts(dve, st, TILES, b_rstd, b_shift, t + 1)
                if mid:
                    dve.wait_ge(b_neg_ready, t)
                    dve.tensor_tensor_scan(b_fill[o][:, ::-1], b_goes[o][:, ::-1], b_neg[:, ::-1],
                                           0.0 if t0 == 1 else b_fill[s][:, 0:1], ALU.mult, ALU.subtract).then_inc(b_fill_ready, 1)
                    dve.wait_ge(b_filter, t)
                    dve.wait_ge(b_w_ld[o], 16 * turn(k, u - 1))
                    dve.scalar_tensor_tensor(out=b_t[:, :], in0=bank[4][:, :], scalar=cols[:, 4:5], in1=b_w[o][:, :],
                                             op0=ALU.add, op1=ALU.mult).then_inc(b_t_ready, 1)
                    dve.wait_ge(b_fill_ready, t)
                    dve.wait_ge(b_t_ready, t)
                    dve.tensor_tensor(b_msg[:, :], b_fill[o][:, :], b_t[:, :], ALU.mult).then_inc(b_msg_ready, 1)
                    dve.wait_ge(b_src_ld[o], 16 * turn(k, u - 1))
                    dve.wait_ge(b_col_ld[o], 16 * turn(k, u - 1))
                    if t0 >= 2:
                        dve.wait_ge(b_summed, t - 1)
                    for j in range(TILES):
                        last = dve.tensor_scalar(b_same[:, j, :], b_src[o][:, :], b_col[o][:, j:j + 1], None, ALU.is_equal)
                    last.then_inc(b_same_ready, 1)
                    dve.wait_ge(b_same_ready, t)
                    for j in range(TILES):
                        last = dve.tensor_tensor(b_before[:, j * P:(j + 1) * P], b_same[:, j, j * P:(j + 1) * P],
                                                 lower[:, j * P:(j + 1) * P], ALU.mult)
                    last.then_inc(b_before_ready, 1)
                if front:
                    dve.wait_ge(b_ln_done, t + 1)
                    dve.scalar_tensor_tensor(out=b_s1[:, :], in0=bank[1][:, :], scalar=0.0, in1=b_ln[:, :],
                                             op0=ALU.max, op1=ALU.add).then_inc(b_s1_ready, 1)
                if mid:
                    dve.wait_ge(b_count, t)
                    dve.scalar_tensor_tensor(out=b_dup[:, :], in0=bank[7][:, 0:TILES], scalar=1.0, in1=b_col[o][:, TILES:2 * TILES],
                                             op0=ALU.min, op1=ALU.mult).then_inc(b_dup_ready, 1)
                    dve.wait_ge(b_dup_ready, t)
                    if t0 >= 3:
                        dve.wait_ge(added[o], 64 * turn(k, u - 3))
                    dve.tensor_tensor(b_at[o][:, :], b_dup[:, :], b_col[o][:, 0:TILES], ALU.add).then_inc(b_at_ready, 1)

            for u in range(4):
                step_b(0, u, u, mid=u >= 1)
            with dve.Fori(2, HALF) as k:
                for u in range(2):
                    step_b(k, u, 4 + u)
            step_b(HALF, 0, 4, front=False)

            def f_ssp(c, q, c0):
                dve.wait_ge(f_ln, c + 1)
                if c0 >= 2:
                    dve.wait_ge(f_y, c - 1)
                dve.scalar_tensor_tensor(out=f_ssp_out[q % 2][:, :], in0=bank[2 + q % 2][:, :], scalar=0.0,
                                         in1=f_ln_out[q % 2][:, :], op0=ALU.max, op1=ALU.add).then_inc(f_s, 1)

            def f_rows(c, q, slot, m, c0):
                dve.wait_ge(f_y, c + 1)
                if q == 0:
                    dve.wait_ge(f_x1_ld[slot], 16 * (m + 1))
                    if c0 >= QUADS * RING_D:
                        dve.wait_ge(out_stored[slot], 16 * m)
                dve.tensor_tensor(d_x1[slot][:, q * 512:(q + 1) * 512], bank[4 + q % 2][:, :],
                                  d_x[slot][:, q * 512:(q + 1) * 512], ALU.add).then_inc(f_out, 1)

            def f_group(g, slot, m, g0):
                for q in range(QUADS):
                    f_ssp(QUADS * g + q, q, QUADS * g0 + q)
                    if q:
                        f_rows(QUADS * g + q - 1, q - 1, slot, m, QUADS * g0 + q - 1)
                    elif g0:
                        f_rows(QUADS * g - 1, QUADS - 1, (slot - 1) % RING_D, m if slot else m - 1, QUADS * g0 - 1)

            for g in range(RING_D + 1):
                f_group(g, g % RING_D, g // RING_D, g)
            for g in range(RING_D + 1, 2 * RING_D):
                f_group(g, g % RING_D, g // RING_D, g) if g < NG else None
            F_LOOPS = NG // RING_D - 2
            if F_LOOPS > 0:
                with dve.Fori(2, 2 + F_LOOPS) as m:
                    for i in range(RING_D):
                        f_group(m * RING_D + i, i, m, 2 * RING_D)
            for g in range(max(2 + F_LOOPS, 2) * RING_D, NG):
                f_group(g, g % RING_D, g // RING_D, g)
            f_rows(QUADS * NG - 1, QUADS - 1, (NG - 1) % RING_D, (NG - 1) // RING_D, QUADS * NG - 1)

        @block.scalar
        def _(act):
            act.preload_act_table_set("natural_log_exp_and_others")
            def step_d(g, slot, front=True, back=True):
                if back:
                    for q in range(QUADS):
                        c = QUADS * (g - 1) + q
                        act.wait_ge(d_turned, c + 1)
                        if not (isinstance(c, int) and c < 2):
                            act.wait_ge(d_mm, c - 1)
                        act.activation(turned[q % 2][:, :], bank[q % 2][:, :], ACT.Relu).then_inc(d_relu, 1)
                if front:
                    inverse_deviation(act, stat_d[0], J, d_var, d_log, d_rstd, g + 1)
                    act.wait_ge(d_shift, g + 1)
                    if not (isinstance(g, int) and g < RING_D):
                        act.wait_ge(d_turned, QUADS * (g - 2))
                    for q in range(QUADS - 1):
                        for j in range(4 * q, 4 * q + 4):
                            last = act.activation(d_n[slot][:, j * F:(j + 1) * F], d_x[slot][:, j * F:(j + 1) * F], ACT.Relu,
                                                  scale=stat_d[0]["rstd"][:, j:j + 1], bias=stat_d[0]["shift"][:, j:j + 1])
                        last.then_inc(d_norm_act, 1)

            for g in range(RING_D):
                step_d(g, g, back=g > 0)
            LOOPS = (NG - RING_D) // RING_D
            with act.Fori(1, 1 + LOOPS) as m:
                for i in range(RING_D):
                    step_d(m * RING_D + i, i)
            for g in range((1 + LOOPS) * RING_D, NG + 1):
                step_d(g, g % RING_D, front=g < NG)

            def step_a(k, u, t0, front=True, mid=True):
                s = u % 2
                o = 1 - s
                t = 2 * k + u
                st = stat_e[s]
                if front:
                    inverse_deviation(act, st, 2 * TILES, var, log_var, rstd, t + 1)
                if mid:
                    act.wait_ge(dif_decay, t)
                    act.activation(a_decay[:, :], a_d1[:, :], ACT.Exp).then_inc(exp_decay, 1)
                    act.wait_ge(dif_score, t)
                    act.activation(a_p[:, :], a_d2[:, :], ACT.Exp).then_inc(exp_score, 1)
                    act.activation(a_ps[:, :], a_max[o][:, 1:C + 1], ACT.Exp, scale=-1.0).then_inc(exp_self, 1)
                if front:
                    act.wait_ge(shift, t + 1)
                    for j in range(TILES):
                        last = act.activation(a_ns[:, j * F:(j + 1) * F], a_xs[s][:, j * F:(j + 1) * F], ACT.Relu,
                                              scale=st["rstd"][:, j:j + 1], bias=st["shift"][:, j:j + 1])
                    last.then_inc(norm_src, 1)
                    act.wait_ge(turned_src, t + 1)
                    if t0 >= 1:
                        act.wait_ge(base_mm, t)
                    act.activation(a_hs[:, :], bank[0][:, :], ACT.Copy).then_inc(h_src, 1)
                    act.wait_ge(turned_dst, t + 1)
                    act.activation(a_hd[:, :], bank[1][:, :], ACT.Relu).then_inc(h_dst, 1)
                if mid:
                    act.wait_ge(den_all, t)
                    act.activation(a_log[:, :], a_all[:, :], ACT.Ln).then_inc(den_log, 1)
                    act.wait_ge(den_log, t)
                    act.activation(a_rec[:, :], a_log[:, :], ACT.Exp, scale=-1.0).then_inc(den_rec, 1)
                if front:
                    act.wait_ge(self_mm, t + 1)
                    if t0 >= 1:
                        act.wait_ge(score_mm, t)
                    act.activation(a_us[:, :], bank[2][:, :], ACT.Relu, bias=cols[:, 3:4]).then_inc(self_relu, 1)
                    act.wait_ge(v_mm, t + 1)
                    act.activation(a_v[s][:, :], bank[3][:, :], ACT.Copy).then_inc(v_copied, 1)
                    act.wait_ge(edge_mm, t + 1)
                    act.activation(a_u[:, :], bank[4][:, :], ACT.Relu, bias=cols[:, 3:4]).then_inc(edge_relu, 1)

            act.wait_ge(weights_ready, 1)
            for u in range(4):
                step_a(0, u, u, mid=u >= 1)
            with act.Fori(2, HALF) as k:
                for u in range(2):
                    step_a(k, u, 4 + u)
            step_a(HALF, 0, 4, front=False)

            def softplus(z, ab, ex, ln, z_done, abs_done, exp_done, ln_done, count):
                act.wait_ge(z_done, count)
                act.activation(ab[:, :], z[:, :], ACT.Abs).then_inc(abs_done, 1)
                act.wait_ge(abs_done, count)
                act.activation(ex[:, :], ab[:, :], ACT.Exp, scale=-1.0).then_inc(exp_done, 1)
                act.wait_ge(exp_done, count)
                act.activation(ln[:, :], ex[:, :], ACT.Ln, scale=0.5, bias=0.5).then_inc(ln_done, 1)

            def step_b(k, u, t0, front=True, mid=True):
                s = u % 2
                t = 2 * k + u
                st = stat_e[s]
                if front:
                    act.wait_ge(b_fa_turned, t + 1)
                    act.activation(b_f[0:RBF, :].rearrange("r (p j) -> r j p", j=TILES),
                                   bank[0][0:RBF, :].rearrange("r (j p) -> r j p", j=TILES), ACT.Copy).then_inc(b_f_ready, 1)
                    inverse_deviation(act, st, TILES, b_var, b_logv, b_rstd, t + 1)
                    act.wait_ge(b_shift, t + 1)
                    for j in range(TILES):
                        last = act.activation(b_n[:, j * F:(j + 1) * F], b_x[s][:, j * F:(j + 1) * F], ACT.Relu,
                                              scale=st["rstd"][:, j:j + 1], bias=st["shift"][:, j:j + 1])
                    last.then_inc(b_norm, 1)
                    if t0 >= 1:
                        act.wait_ge(b_s1_ready, t)
                    softplus(bank[1], b_abs, b_exp, b_ln, b_z1, b_abs_done, b_exp_done, b_ln_done, t + 1)
                if mid:
                    act.wait_ge(b_msg_turned, t)
                    if t0 >= 2:
                        act.wait_ge(b_summed, t - 1)
                    act.activation(b_rows[:, :], bank[5][:, :], ACT.Copy).then_inc(b_rows_ready, 1)
                if front:
                    act.wait_ge(b_turned, t + 1)
                    act.activation(b_h[:, :], bank[2][:, :], ACT.Copy).then_inc(b_h_ready, 1)
                if mid:
                    act.wait_ge(b_summed, t)
                    if t0 >= 3:
                        act.wait_ge(added[1 - s], 64 * turn(k, u - 3))
                    act.activation(b_sum[1 - s][:, :], bank[6][:, :], ACT.Copy).then_inc(b_sum_ready, 1)

            act.wait_ge(ones_set, 1)
            for u in range(4):
                step_b(0, u, u, mid=u >= 1)
            with act.Fori(2, HALF) as k:
                for u in range(2):
                    step_b(k, u, 4 + u)
            step_b(HALF, 0, 4, front=False)

            def f_copy(c, q, c0):
                act.wait_ge(f_turned, c + 1)
                if c0 >= 2:
                    act.wait_ge(f_z, c - 1)
                act.activation(turned[q % 2][:, :], bank[q % 2][:, :], ACT.Copy).then_inc(f_copied, 1)

            def f_network(c, q, c0):
                if c0 >= 2:
                    act.wait_ge(f_s, c - 1)
                softplus(bank[2 + q % 2], f_abs_out, f_exp_out, f_ln_out[q % 2], f_z, f_abs, f_exp, f_ln, c + 1)

            def f_group(g, g0):
                for q in range(QUADS):
                    f_copy(QUADS * g + q, q, QUADS * g0 + q)
                    if g0 or q:
                        f_network(QUADS * g + q - 1, q - 1, QUADS * g0 + q - 1)

            f_group(0, 0)
            with act.Fori(1, NG) as g:
                f_group(g, 1)
            f_network(QUADS * NG - 1, QUADS - 1, QUADS * NG - 1)

        @block.tensor
        def _(pe):
            def turn_tiles(to, tiles, n=TILES, width=F):
                for j in range(n):
                    last = pe.transpose(to[0:width, j * P:(j + 1) * P], tiles[:, j * width:(j + 1) * width], ident[:, :])
                return last

            pe.wait_ge(pool_const, 1)
            pe.wait_ge(index_f_ready, 1)
            for i, a in enumerate((rawf[:, 0, :], gather_f[:, :], scatter_f[:, :])):
                for j in range(TILES):
                    last = pe.transpose(bank[i][:, j * NC:(j + 1) * NC], a[0:NC, j * P:(j + 1) * P], ident[0:NC, 0:NC])
                last.then_inc(index_turned, 1)
            pe.wait_ge(parts, 1)
            pe.wait_ge(index_ready, 3)

            def d_turn(g, slot, q):
                c = QUADS * g + q
                if q < QUADS - 1:
                    pe.wait_ge(d_norm_act, 3 * g + q + 1)
                else:
                    pe.wait_ge(d_norm_dve, g + 1)
                if not (isinstance(c, int) and c < 2):
                    pe.wait_ge(d_relu, c - 1)
                turn_tiles(bank[q % 2], d_n[slot][:, q * 512:(q + 1) * 512]).then_inc(d_turned, 1)

            def d_multiply(g, q):
                c = QUADS * g + q
                to = bank[2 + q % 2]
                if not (isinstance(c, int) and c < 2):
                    pe.wait_ge(d_x1_ready, c - 1)
                pe.matmul(to[:, :], ones3[:, 0:P], bias3[:, :, :].rearrange("k j f -> k (j f)"), start=True, stop=False)
                pe.wait_ge(d_relu, c + 1)
                for j in range(4):
                    last = pe.matmul(to[:, j * F:(j + 1) * F], turned[q % 2][:, j * P:(j + 1) * P], wl[:, :],
                                     start=False, stop=(j == 3))
                last.then_inc(d_mm, 1)

            def step_d(g, slot):
                d_turn(g, slot, 0)
                for q in range(1, QUADS):
                    d_turn(g, slot, q)
                    d_multiply(g, q - 1)
                d_multiply(g, QUADS - 1)

            step_d(0, 0)
            LOOPS = (NG - 1) // RING_D
            with pe.Fori(0, LOOPS) as m:
                for i in range(RING_D):
                    step_d(m * RING_D + i + 1, (i + 1) % RING_D)
            for g in range(1 + LOOPS * RING_D, NG):
                step_d(g, g % RING_D)

            pe.wait_ge(weights_ready, 1)

            def step_a(k, u, t0, front=True, back=True):
                s = u % 2
                t = 2 * k + u
                if back:
                    pe.wait_ge(att_out, t - 1)
                    if t0 >= 3:
                        pe.wait_ge(x1_ready, t - 2)
                    turn_tiles(bank[7], a_o[s]).then_inc(out_turned, 1)
                if front:
                    pe.wait_ge(norm_src, t + 1)
                    if t0 >= 1:
                        pe.wait_ge(h_dst, t)
                    turn_tiles(bank[0], a_ns).then_inc(turned_src, 1)
                    pe.wait_ge(norm_dst, t + 1)
                    turn_tiles(bank[1], a_nd).then_inc(turned_dst, 1)
                    pe.wait_ge(h_dst, t + 1)
                    if t0 >= 1:
                        pe.wait_ge(edge_relu, t)
                    pe.matmul(bank[2][:, :], wlr[:, :], a_hd[:, :], start=True, stop=True).then_inc(self_mm, 1)
                    pe.matmul(bank[3][:, :], neg_wl[:, :], a_hd[:, :], start=True, stop=False)
                    pe.matmul(bank[3][:, :], wl[:, :], a_hs[:, :], start=False, stop=True).then_inc(v_mm, 1)
                    pe.matmul(bank[4][:, :], wl[:, :], a_hs[:, :], start=True, stop=False)
                    pe.matmul(bank[4][:, :], wr[:, :], a_hd[:, :], start=False, stop=True).then_inc(edge_mm, 1)
                    if t0 >= 1:
                        pe.wait_ge(base_ready, t)
                    pe.matmul(bank[6][:, :], ones3[:, 0:P], bias3[:, :, :].rearrange("k j f -> k (j f)"), start=True, stop=False)
                    for j in range(TILES):
                        last = pe.matmul(bank[6][:, j * F:(j + 1) * F], a_hd[:, j * P:(j + 1) * P], wl[:, :],
                                         start=False, stop=(j == TILES - 1))
                    last.then_inc(base_mm, 1)
                    if t0 >= 1:
                        pe.wait_ge(dif_score, t)
                    pe.wait_ge(self_relu, t + 1)
                    pe.matmul(bank[5][:, :], neg_att_relu[:, :], a_us[:, :], start=True, stop=False)
                    pe.wait_ge(v_copied, t + 1)
                    pe.matmul(bank[5][:, :], att_lin[:, :], a_v[s][:, :], start=False, stop=False)
                    pe.wait_ge(edge_relu, t + 1)
                    pe.matmul(bank[5][:, :], att_relu[:, :], a_u[:, :], start=False, stop=True).then_inc(score_mm, 1)

            for u in range(4):
                step_a(0, u, u, back=u >= 2)
            with pe.Fori(2, HALF) as k:
                for u in range(2):
                    step_a(k, u, 4 + u)
            for u in range(2):
                step_a(HALF, u, 4 + u, front=False)

            def step_b(k, u, t0, front=True, mid=True):
                s = u % 2
                t = 2 * k + u
                if front:
                    pe.wait_ge(b_fa_ld[s], 16 * turn(k, u))
                    if t0 >= 1:
                        pe.wait_ge(b_f_ready, t)
                    turn_tiles(bank[0], b_fa[s], width=RBF).then_inc(b_fa_turned, 1)
                    pe.wait_ge(b_f_ready, t + 1)
                    if t0 >= 1:
                        pe.wait_ge(b_s1_ready, t)
                    pe.matmul(bank[1][:, :], wf1[0:RBF + 1, :], b_f[0:RBF + 1, :], start=True, stop=True).then_inc(b_z1, 1)
                    pe.wait_ge(b_norm, t + 1)
                    if t0 >= 1:
                        pe.wait_ge(b_h_ready, t)
                    turn_tiles(bank[2], b_n).then_inc(b_turned, 1)
                if mid:
                    pe.wait_ge(b_msg_ready, t)
                    if t0 >= 2:
                        pe.wait_ge(b_rows_ready, t - 1)
                    turn_tiles(bank[5], b_msg).then_inc(b_msg_turned, 1)
                if front:
                    pe.wait_ge(b_h_ready, t + 1)
                    if t0 >= 1:
                        pe.wait_ge(b_neg_ready, t)
                    pe.matmul(bank[3][:, :], win[:, :], b_h[:, :], start=True, stop=True).then_inc(b_hf, 1)
                if mid:
                    pe.wait_ge(b_before_ready, t)
                    if t0 >= 2:
                        pe.wait_ge(b_dup_ready, t - 1)
                    for i in range(TILES):
                        for j in range(i):
                            pe.matmul(bank[7][:, i:i + 1], b_same[:, j, i * P:(i + 1) * P], ones[:, 0:1], start=(j == 0), stop=False)
                        last = pe.matmul(bank[7][:, i:i + 1], b_before[:, i * P:(i + 1) * P], ones[:, 0:1], start=(i == 0), stop=True)
                    last.then_inc(b_count, 1)
                    pe.wait_ge(b_rows_ready, t)
                    if t0 >= 2:
                        pe.wait_ge(b_sum_ready, t - 1)
                    for i in range(TILES):
                        for j in range(TILES):
                            last = pe.matmul(bank[6][:, i * F:(i + 1) * F], b_same[:, j, i * P:(i + 1) * P],
                                             b_rows[:, j * F:(j + 1) * F], start=(j == 0), stop=(j == TILES - 1))
                    last.then_inc(b_summed, 1)
                if front:
                    pe.wait_ge(b_s1_ready, t + 1)
                    if t0 >= 1:
                        pe.wait_ge(b_t_ready, t)
                    pe.matmul(bank[4][:, :], wf2[:, :], b_s1[:, :], start=True, stop=True).then_inc(b_filter, 1)

            for u in range(4):
                step_b(0, u, u, mid=u >= 1)
            with pe.Fori(2, HALF) as k:
                for u in range(2):
                    step_b(k, u, 4 + u)
            step_b(HALF, 0, 4, front=False)

            def f_turn(c, q, slot, m, c0):
                if q == 0:
                    pe.wait_ge(f_sum_ld[slot], 16 * (m + 1))
                if c0 >= 2:
                    pe.wait_ge(f_copied, c - 1)
                turn_tiles(bank[q % 2], d_n[slot][:, q * 512:(q + 1) * 512]).then_inc(f_turned, 1)

            def f_first(c, q, c0):
                pe.wait_ge(f_copied, c + 1)
                if c0 >= 2:
                    pe.wait_ge(f_s, c - 1)
                to = bank[2 + q % 2]
                pe.matmul(to[:, :], bo13[:, :], ones3[:, :], start=True, stop=False)
                pe.matmul(to[:, :], wo1[:, :], turned[q % 2][:, :], start=False, stop=True).then_inc(f_z, 1)

            def f_second(c, q, c0):
                if c0 >= 2:
                    pe.wait_ge(f_out, c - 1)
                to = bank[4 + q % 2]
                pe.matmul(to[:, :], ones3[:, 0:P], bo23[:, :, :].rearrange("k j f -> k (j f)"), start=True, stop=False)
                pe.wait_ge(f_s, c + 1)
                for j in range(TILES):
                    last = pe.matmul(to[:, j * F:(j + 1) * F], f_ssp_out[q % 2][:, j * P:(j + 1) * P], wo2[:, :],
                                     start=False, stop=(j == TILES - 1))
                last.then_inc(f_y, 1)

            def f_group(g, slot, m, g0):
                for q in range(QUADS):
                    c, c0 = QUADS * g + q, QUADS * g0 + q
                    f_turn(c, q, slot, m, c0)
                    if c0 >= 2:
                        f_second(c - 2, q - 2, c0 - 2)
                    if c0 >= 1:
                        f_first(c - 1, q - 1, c0 - 1)

            for g in range(RING_D):
                f_group(g, g, 0, g)
            F_LOOPS = NG // RING_D - 1
            if F_LOOPS:
                with pe.Fori(1, 1 + F_LOOPS) as m:
                    for i in range(RING_D):
                        f_group(m * RING_D + i, i, m, RING_D)
            for g in range((1 + F_LOOPS) * RING_D, NG):
                f_group(g, g % RING_D, g // RING_D, g)
            c = QUADS * NG
            f_first(c - 1, QUADS - 1, c - 1)
            f_second(c - 2, QUADS - 2, c - 2)
            f_second(c - 1, QUADS - 1, c - 1)


_INS = ['x', 'src', 'dst', 'edge_attr_20', 'edge_weight', 'L0_gnn_W_l', 'L0_gnn_b_l', 'L0_gnn_W_r', 'L0_gnn_b_r',
        'L0_gnn_att', 'L0_gnn_bias', 'L1_gnn_W_in2f', 'L1_gnn_Wf1', 'L1_gnn_bf1', 'L1_gnn_Wf2', 'L1_gnn_bf2',
        'L1_gnn_Wo1', 'L1_gnn_bo1', 'L1_gnn_Wo2', 'L1_gnn_bo2']


def kernel(**inputs):
    import numpy as _np
    import concourse.bacc as _bacc
    from concourse import mybir as _mybir
    from concourse.bass_utils import run_bass_kernel_spmd as _run

    nc = _bacc.Bacc("TRN2", target_bir_lowering=False, num_devices=1)
    arrays, args = {}, []
    for name in _INS:
        a = _np.ascontiguousarray(inputs[name])
        arrays[f"in_{name}"] = a
        args.append(nc.dram_tensor(f"in_{name}", a.shape, _mybir.dt.from_np(a.dtype), kind="ExternalInput").ap())
    out = nc.dram_tensor("out", inputs['x'].shape, _mybir.dt.float32, kind="ExternalOutput").ap()
    gnn(nc, *args, out)
    r = _run(nc, [arrays], core_ids=[0])
    return r.results[0]["out"]
```

```python
from contextlib import ExitStack

import concourse.bass as bass
from concourse import mybir

P = 128
F = 128
HEADS = 4
HC = F // HEADS
TILES = 4
C = TILES * P
J = 16
GROUP = J * P
QUADS = J // 4
J_ACT = J - 2
DST_ACT = 0
RX = 4
RN = 2
EPS = 1e-5
SLOPE = 0.2
SKIP = 1 << 20

ALU = mybir.AluOpType
ACT = mybir.ActivationFunctionType
F32 = mybir.dt.float32
BF16 = mybir.dt.bfloat16
I32 = mybir.dt.int32


def turn(k, u):
    return k + u // 2 + 1


def gnn(nc, x, src, dst, edge_attr, edge_weight, W_l, b_l, W_r, b_r, att, bias,
        W_in, Wf1, bf1, Wf2, bf2, Wo1, bo1, Wo2, bo2, out):
    N = x.shape[0]
    E = src.shape[0]
    RBF = edge_attr.shape[1]
    NC = -(-E // C)
    NC += NC % 2
    NG = -(-N // GROUP)
    FULL = E // C
    REST = E - FULL * C
    assert NG == NC // 2
    assert REST and NC == FULL + 1 and NC <= P and NC >= 6 and NG >= 4

    x1_dram = nc.dram_tensor("x1_dram", (N, F), F32).ap()
    x1_end_dram = nc.dram_tensor("x1_end_dram", (NC, P, TILES * F), F32).ap()
    sum_dram = nc.dram_tensor("sum_dram", (N + C, F), F32).ap()
    goes_dram = nc.dram_tensor("goes_dram", (NC, C), BF16).ap()
    src_dram = nc.dram_tensor("src_dram", (NC, C), F32).ap()
    keep_dram = nc.dram_tensor("keep_dram", (NC, C), BF16).ap()
    weight_dram = nc.dram_tensor("weight_dram", (NC, C), F32).ap()
    attr_dram = nc.dram_tensor("attr_dram", (NC * C, RBF), F32).ap()

    with ExitStack() as ctx:
        def sb(name, shape, dt=F32):
            return ctx.enter_context(nc.sbuf_tensor(name, shape, dt))

        def two(name, shape, dt=F32):
            return [sb(f"{name}{i}", shape, dt) for i in range(2)]

        def sem(name):
            return ctx.enter_context(nc.semaphore(name))

        def sems(name, n=2):
            return [sem(f"{name}{i}") for i in range(n)]

        bank = [ctx.enter_context(nc.psum_tensor(f"bank{i}", [P, 512], F32)) for i in range(8)]

        wl = sb("wl", [P, F]); neg_wl = sb("neg_wl", [P, F]); wr = sb("wr", [P, F]); wlr = sb("wlr", [P, F])
        win = sb("win", [P, F]); wf1 = sb("wf1", [32, F]); wf2 = sb("wf2", [P, F])
        wo1 = sb("wo1", [P, F]); wo2 = sb("wo2", [P, F])
        ident = sb("ident", [P, P])
        heads = sb("heads", [P, F])
        att_relu = sb("att_relu", [P, F])
        neg_att_relu = sb("neg_att_relu", [P, F])
        att_lin = sb("att_lin", [P, F])
        cols = sb("cols", [P, 8])
        bo1_3 = sb("bo1_3", [P, 3])
        rows3 = sb("rows3", [3, 3 * F])
        part3 = sb("part3", [3, 3, 2 * F])
        part3b = sb("part3b", [3, 2, 2 * F], BF16)
        sel3 = sb("sel3", [3, 2, 2 * F])
        bias3 = sb("bias3", [3, 4, F], BF16)
        bo23 = sb("bo23", [3, 4, F], BF16)
        ones3 = sb("ones3", [3, 512], BF16)
        index = sb("index", [P, 12 * NC], I32)
        columns = sb("columns", [P, 8 * NC])
        dump = sb("dump", [P, TILES])
        dump_i = sb("dump_i", [P, TILES], I32)
        lower = sb("lower", [P, TILES * P])
        clear_rows = N + C - (NG - 1) * GROUP
        zero = sb("zero", [P, clear_rows])

        def ring(name, n):
            return [sb(f"{name}{i}", [P, J * F]) for i in range(n)]

        d_x = ring("d_x", RX)
        d_n = ring("d_n", RN)
        d_x1 = ring("d_x1", RN)
        turned = [sb(f"turned{i}", [P, 512]) for i in range(2)]

        with ExitStack() as place:
            def at(name, shape, dt=F32):
                return place.enter_context(nc.sbuf_tensor(name, shape, dt))

            raw = at("raw", [P, 4, C], I32)
            rawf = at("rawf", [P, 4, C])
            goes_f = at("goes_f", [P, C])
            goes_b = at("goes_b", [P, C], BF16)
            keep_b = at("keep_b", [P, C], BF16)
            gather_f = at("gather_f", [P, C])
            scatter_f = at("scatter_f", [P, C])
            weight_f = at("weight_f", [P, C])
        with ExitStack() as place:
            def at2(name, shape, dt=F32):
                return [at(f"{name}{i}", shape, dt) for i in range(2)]

            b_x = at2("b_x", [P, TILES * F])
            b_fa = at2("b_fa", [P, TILES * RBF])
            b_goes = at2("b_goes", [P, C], BF16)
            b_w = at2("b_w", [P, C])
            b_src = at2("b_src", [P, C])
            b_n = at("b_n", [P, TILES * F])
            b_h = at("b_h", [P, C])
            b_f = at("b_f", [32, C])
            b_abs = at("b_abs", [P, C])
            b_exp = at("b_exp", [P, C])
            b_ln = at("b_ln", [P, C])
            b_s1 = at("b_s1", [P, C])
            b_neg = at("b_neg", [P, C])
            b_fill = at2("b_fill", [P, C])
            b_t = at("b_t", [P, C])
            b_msg = at("b_msg", [P, C])
            b_rows = at2("b_rows", [P, 3, TILES * F], BF16)
            b_rest = at("b_rest", [P, TILES * F])
            b_same = at2("b_same", [P, TILES, C], BF16)
            b_before = at("b_before", [P, TILES * P], BF16)
            b_sum = at2("b_sum", [P, TILES * F])
            b_dup = at("b_dup", [P, TILES])
            b_at = at2("b_at", [P, TILES], I32)
            b_col = at2("b_col", [P, 2 * TILES])
        a_xs = two("a_xs", [P, TILES * F])
        a_xd = two("a_xd", [P, TILES * F])
        a_ns = sb("a_ns", [P, TILES * F])
        a_nd = sb("a_nd", [P, TILES * F])
        a_hs = sb("a_hs", [P, C])
        a_hd = sb("a_hd", [P, C])
        a_us = sb("a_us", [P, C])
        a_u = sb("a_u", [P, C])
        a_v = two("a_v", [P, C])
        a_keep = two("a_keep", [P, C], BF16)
        a_max = two("a_max", [P, C + 1])
        a_d1 = sb("a_d1", [P, C])
        a_d2 = sb("a_d2", [P, C])
        a_decay = sb("a_decay", [P, C])
        a_p = sb("a_p", [P, C])
        a_ps = sb("a_ps", [P, C])
        a_dec = sb("a_dec", [P, C])
        a_pv = sb("a_pv", [P, C])
        a_den = two("a_den", [P, C])
        a_sum = two("a_sum", [P, C])
        a_all = sb("a_all", [P, C])
        a_log = sb("a_log", [P, C])
        a_rec = sb("a_rec", [P, C])
        a_o = two("a_o", [P, C])
        a_base = two("a_base", [P, TILES * F])
        a_x1 = two("a_x1", [P, TILES * F])
        ones = sb("ones", [P, 1], BF16)
        f_abs_out = sb("f_abs_out", [P, 512]); f_exp_out = sb("f_exp_out", [P, 512])
        f_ln_out = two("f_ln_out", [P, 512]); f_ssp_out = two("f_ssp_out", [P, 512])

        def stat(name, n, rings):
            return [{"six": sb(f"{name}_six{i}", [P, n, 6]),
                     "sum": sb(f"{name}_sum{i}", [P, n]),
                     "dif": sb(f"{name}_dif{i}", [P, n]),
                     "sq": sb(f"{name}_sq{i}", [P, n]),
                     "sq2": sb(f"{name}_sq2{i}", [P, n]),
                     "var": sb(f"{name}_var{i}", [P, n]),
                     "log": sb(f"{name}_log{i}", [P, n]),
                     "rstd": sb(f"{name}_rstd{i}", [P, n]),
                     "shift": sb(f"{name}_shift{i}", [P, n])}
                    for i in range(rings)]

        stat_d = stat("stat_d", J, 2)
        stat_e = stat("stat_e", 2 * TILES, 2)

        gidx = [sb(f"gidx{i}", [P, 8], I32) for i in range(2)]
        sidx = [sb(f"sidx{i}", [P, 4], I32) for i in range(2)]

        load_const = sem("load_const"); pool_const = sem("pool_const")
        pads_set = sem("pads_set"); load_raw = sem("load_raw"); load_weight = sem("load_weight")
        pool_step = sem("pool_step"); sync_step = sem("sync_step")
        setup = sem("setup")
        weights_ready = sem("weights_ready"); columns_ready = sem("columns_ready"); zero_set = sem("zero_set")
        keep_ready = sem("keep_ready"); index_f_ready = sem("index_f_ready"); index_turned = sem("index_turned")
        index_ready = sem("index_ready"); store_setup = sem("store_setup"); parts = sem("parts"); bo1_ready = sem("bo1_ready")

        xd_loaded = sems("xd_loaded", RX); x1_stored = sems("x1_stored", RN)
        d_six = sem("d_six"); d_sumdif = sem("d_sumdif"); d_sq = sem("d_sq"); d_var = sem("d_var")
        d_log = sem("d_log"); d_rstd = sem("d_rstd"); d_shift = sem("d_shift")
        d_norm_act = sem("d_norm_act"); d_norm_dve = sem("d_norm_dve")
        d_turned = sem("d_turned"); d_relu = sem("d_relu"); d_mm = sem("d_mm"); d_x1_ready = sem("d_x1_ready")

        gidx_loaded = sems("gidx_loaded"); keep_loaded = sems("keep_loaded")
        src_gathered = sems("src_gathered"); dst_gathered = sems("dst_gathered")
        cleared = sem("cleared"); end_stored = sems("end_stored")
        six = sem("six"); sumdif = sem("sumdif"); sq = sem("sq"); var = sem("var")
        log_var = sem("log_var"); rstd = sem("rstd"); shift = sem("shift")
        norm_src = sem("norm_src"); norm_dst = sem("norm_dst")
        turned_src = sem("turned_src"); turned_dst = sem("turned_dst")
        h_dst = sem("h_dst")
        self_mm = sem("self_mm"); v_mm = sem("v_mm"); edge_mm = sem("edge_mm"); base_mm = sem("base_mm")
        self_relu = sem("self_relu"); v_copied = sem("v_copied"); edge_relu = sem("edge_relu")
        score_mm = sem("score_mm"); max_carry = sem("max_carry"); max_scan = sem("max_scan")
        dif_decay = sem("dif_decay"); dif_score = sem("dif_score")
        exp_decay = sem("exp_decay"); exp_score = sem("exp_score"); exp_self = sem("exp_self")
        decay = sem("decay"); weighted = sem("weighted"); den_scan = sem("den_scan"); sum_scan = sem("sum_scan")
        den_all = sem("den_all"); den_log = sem("den_log"); den_rec = sem("den_rec")
        base_ready = sem("base_ready"); att_out = sem("att_out"); out_turned = sem("out_turned")
        x1_ready = sem("x1_ready")

        b_x_ld = sems("b_x_ld"); b_fa_ld = sems("b_fa_ld"); b_goes_ld = sems("b_goes_ld"); b_w_ld = sems("b_w_ld")
        b_src_ld = sems("b_src_ld"); b_sidx_ld = sems("b_sidx_ld"); b_col_ld = sems("b_col_ld")
        x1_scattered = sems("x1_scattered"); added = sems("added")
        ones_set = sem("ones_set"); b_six = sem("b_six"); b_sumdif = sem("b_sumdif"); b_sq = sem("b_sq")
        b_var = sem("b_var"); b_logv = sem("b_logv"); b_rstd = sem("b_rstd"); b_shift = sem("b_shift")
        b_norm = sem("b_norm")
        b_fa_turned = sem("b_fa_turned"); b_f_ready = sem("b_f_ready"); b_z1 = sem("b_z1")
        b_abs_done = sem("b_abs_done"); b_exp_done = sem("b_exp_done"); b_ln_done = sem("b_ln_done")
        b_s1_ready = sem("b_s1_ready"); b_turned = sem("b_turned"); b_h_ready = sem("b_h_ready")
        b_hf = sem("b_hf"); b_filter = sem("b_filter"); b_neg_ready = sem("b_neg_ready")
        b_fill_ready = sem("b_fill_ready"); b_t_ready = sem("b_t_ready"); b_msg_ready = sem("b_msg_ready")
        b_msg_turned = sem("b_msg_turned"); b_part1 = sem("b_part1"); b_rest1 = sem("b_rest1"); b_part2 = sem("b_part2"); b_part3 = sem("b_part3"); b_same_ready = sem("b_same_ready")
        b_before_ready = sem("b_before_ready"); b_count = sem("b_count"); b_dup_ready = sem("b_dup_ready")
        b_at_ready = sem("b_at_ready"); b_summed = sem("b_summed"); b_sum_ready = sem("b_sum_ready")

        f_x1_ld = sems("f_x1_ld", RX); f_sum_ld = sems("f_sum_ld", RN); out_stored = sems("out_stored", RN)
        f_turned = sem("f_turned"); f_copied = sem("f_copied"); f_z = sem("f_z"); f_abs = sem("f_abs")
        f_exp = sem("f_exp"); f_ln = sem("f_ln"); f_s = sem("f_s"); f_y = sem("f_y"); f_out = sem("f_out")

        N_CONST = 16
        N_RAW = 9
        in_slot = [len(range(i, NG, RN)) for i in range(RN)]
        HALF = NC // 2
        bound = N - 1
        ROUNDS = (NG - 1 - RX) // RX

        def node_rows(a, g):
            start = g * GROUP if not isinstance(g, int) or g < NG - 1 else N - GROUP
            return a[bass.ds(start, GROUP), :].rearrange("(p j) f -> p (j f)", p=P)

        block = ctx.enter_context(nc.Block())

        @block.sync
        def _(sp):
            def const(tile, a):
                sp.dma_start(tile, a).then_inc(load_const, 16)

            for tile, a in ((wl, W_l), (wr, W_r), (win, W_in), (wf2, Wf2), (wo1, Wo1), (wo2, Wo2)):
                const(tile[:, :], a)
            const(wf1[0:RBF, :], Wf1)
            const(wf1[RBF:RBF + 1, :], bf1.rearrange("(a f) -> a f", a=1))
            const(cols[:, 0:1], att.rearrange("h (c o) -> (h c) o", o=1))
            for n, a in enumerate((b_l, b_r)):
                const(cols[:, 1 + n:2 + n], a.rearrange("(f o) -> f o", o=1))
            for n, a in enumerate((bf2, bo1)):
                const(cols[:, 4 + n:5 + n], a.rearrange("(f o) -> f o", o=1))
            for n, a in enumerate((b_l, bias, bo2)):
                const(rows3[:, n * F:(n + 1) * F], a.rearrange("(a f) -> a f", a=1).broadcast_to([3, F]))
            sp.wait_ge(pads_set, 1)

            def by_chunk(i, r0, r1, a):
                sp.dma_start(raw[r0:r1, i, :], a.rearrange("(r c) -> r c", c=C)).then_inc(load_raw, 16)

            def part(i, r, c0, a):
                sp.dma_start(raw[r:r + 1, i, c0:c0 + a.shape[0]], a.rearrange("(o c) -> o c", o=1)).then_inc(load_raw, 16)

            by_chunk(0, 0, FULL, src[0:FULL * C])
            part(0, FULL, 0, src[FULL * C:E])
            by_chunk(1, 0, FULL, dst[0:FULL * C])
            part(1, FULL, 0, dst[FULL * C:E])
            by_chunk(2, 0, FULL, dst[1:FULL * C + 1])
            part(2, FULL, 0, dst[FULL * C + 1:E])
            part(3, 0, 1, dst[0:C - 1])
            by_chunk(3, 1, FULL, dst[C - 1:FULL * C - 1])
            part(3, FULL, 0, dst[FULL * C - 1:E - 1])
            sp.dma_start(weight_f[0:FULL, :], edge_weight[0:FULL * C].rearrange("(r c) -> r c", c=C)).then_inc(load_weight, 16)
            sp.dma_start(weight_f[FULL:NC, 0:REST], edge_weight[FULL * C:E].rearrange("(r c) -> r c", r=1)).then_inc(load_weight, 16)
            for g in range(RX):
                sp.dma_start(d_x[g][:, :], node_rows(x, g)).then_inc(xd_loaded[g], 16)
            sp.wait_ge(zero_set, 1)
            flat = attr_dram.rearrange("e r -> (e r)")
            sp.dma_start(flat[0:E * RBF].rearrange("(a b) -> a b", a=400),
                         edge_attr.rearrange("e r -> (e r)").rearrange("(a b) -> a b", a=400)).then_inc(store_setup, 16)
            pad_rows = (NC * C - E) * RBF // 32
            sp.dma_start(flat[E * RBF:NC * C * RBF].rearrange("(a b) -> a b", b=32), zero[0:pad_rows, 0:32]).then_inc(store_setup, 16)
            sp.wait_ge(load_weight, 32)
            sp.dma_start(weight_dram, weight_f[0:NC, :]).then_inc(store_setup, 16)
            sp.wait_ge(keep_ready, 3)
            sp.dma_start(keep_dram, keep_b[0:NC, :]).then_inc(store_setup, 16)
            sp.dma_start(goes_dram, goes_b[0:NC, :]).then_inc(store_setup, 16)
            sp.dma_start(src_dram, rawf[0:NC, 0, :]).then_inc(store_setup, 16)

            def load(g, slot):
                sp.dma_start(d_x[slot][:, :], node_rows(x, g)).then_inc(xd_loaded[slot], 16)

            def store(g, slot):
                sp.wait_ge(d_x1_ready, QUADS * g + QUADS)
                sp.dma_start(node_rows(x1_dram, g), d_x1[slot % RN][:, :]).then_inc(x1_stored[slot % RN], 16)

            with sp.Fori(0, ROUNDS) as m:
                for i in range(RX):
                    store(m * RX + i, i)
                    load(m * RX + i + RX, i)
            for g in range(ROUNDS * RX, NG):
                if g == NG - 1:
                    sp.wait_ge(x1_stored[(g - 1) % RN], 16 * in_slot[(g - 1) % RN])
                store(g, g % RX)
                if g + RX < NG:
                    load(g + RX, g % RX)

            sp.wait_ge(store_setup, 96)
            sp.wait_ge(index_ready, 3)
            sum_flat = sum_dram.rearrange("n f -> (n f)")

            def clear(k):
                if isinstance(k, int) and k == NG - 1:
                    sp.dma_start(sum_flat[k * GROUP * F:(N + C) * F].rearrange("(p m) -> p m", p=P), zero[:, :]).then_inc(cleared, 16)
                else:
                    sp.dma_start(sum_flat[bass.ds(k * GROUP * F, GROUP * F)].rearrange("(p m) -> p m", p=P),
                                 zero[:, 0:J * F]).then_inc(cleared, 16)

            def load_gidx(k, u):
                s = u % 2
                sp.dma_start(gidx[s][:, :], index[:, bass.ds(12 * (2 * k + u), 8)]).then_inc(gidx_loaded[s], 16)

            def step_a(k, u, t0, gather=True, keep=True, end=True):
                s = u % 2
                if gather:
                    sp.wait_ge(src_gathered[s], 64 * turn(k, u))
                    sp.wait_ge(dst_gathered[s], 64 * turn(k, u))
                    load_gidx(k, u + 2)
                if keep:
                    if t0 >= 2:
                        sp.wait_ge(sum_scan, 2 * k + u - 1)
                    sp.dma_start(a_keep[s][:, :], keep_dram[bass.ds(2 * k + u, 1), :].broadcast_to([P, C])).then_inc(keep_loaded[s], 16)
                if end and t0 >= 3:
                    sp.wait_ge(x1_ready, 2 * k + u - 2)
                    sp.dma_start(x1_end_dram[bass.ds(2 * k + u - 3, 1), :, :].rearrange("o p f -> (o p) f"),
                                 a_x1[1 - s][:, :]).then_inc(end_stored[1 - s], 16)

            load_gidx(0, 0)
            load_gidx(0, 1)
            for u in range(4):
                step_a(0, u, u)
                if u % 2:
                    clear(u // 2)
            with sp.Fori(2, HALF - 1) as k:
                for u in range(2):
                    step_a(k, u, 4 + u)
                clear(k)
            for u in range(5):
                step_a(HALF - 1, u, 4 + u, gather=False, keep=u < 2)
            clear(HALF - 1)

            for s in range(2):
                sp.wait_ge(end_stored[s], 16 * HALF)
            sp.wait_ge(columns_ready, 1)

            def load_rows_b(k, u, t0):
                s = u % 2
                t = 2 * k + u
                if t0 >= 2:
                    sp.wait_ge(x1_scattered[s], 64 * turn(k, u - 2))
                    sp.sem_inc(sync_step, 1)
                    sp.wait_ge(b_norm, t - 1)
                    sp.sem_inc(sync_step, 1)
                sp.dma_start(b_x[s][:, :], x1_end_dram[bass.ds(NC - 1 - t, 1), :, :].rearrange("o p f -> (o p) f")).then_inc(b_x_ld[s], 16)
                sp.dma_start(sidx[s][:, :], index[:, bass.ds(12 * (NC - 1 - t) + 8, 4)]).then_inc(b_sidx_ld[s], 16)
                if t0 >= 2:
                    sp.wait_ge(b_fa_turned, t - 1)
                    sp.sem_inc(sync_step, 1)
                sp.dma_start(b_fa[s][:, :], attr_dram[bass.ds((NC - 1 - t) * C, C), :].rearrange("(p j) r -> p (j r)", p=P)).then_inc(b_fa_ld[s], 16)

            def step_b(k, u, t0, ahead=True):
                s = u % 2
                t = 2 * k + u
                if ahead:
                    load_rows_b(k, u + 1, t0 + 1)
                if t0 >= 2:
                    sp.wait_ge(b_msg_ready, t - 1)
                    sp.sem_inc(sync_step, 1)
                sp.dma_start(b_goes[s][:, :], goes_dram[bass.ds(NC - 1 - t, 1), :].broadcast_to([P, C])).then_inc(b_goes_ld[s], 16)
                sp.dma_start(b_w[s][:, :], weight_dram[bass.ds(NC - 1 - t, 1), :].broadcast_to([P, C])).then_inc(b_w_ld[s], 16)
                if t0 >= 2:
                    sp.wait_ge(b_at_ready, t - 1)
                    sp.sem_inc(sync_step, 1)
                sp.dma_start(b_src[s][:, :], src_dram[bass.ds(NC - 1 - t, 1), :].broadcast_to([P, C])).then_inc(b_src_ld[s], 16)
                sp.dma_start(b_col[s][:, :], columns[:, bass.ds(8 * (NC - 1 - t), 8)]).then_inc(b_col_ld[s], 16)

            load_rows_b(0, 0, 0)
            for u in range(4):
                step_b(0, u, u)
            with sp.Fori(2, HALF - 1) as k:
                for u in range(2):
                    step_b(k, u, 4 + u)
            step_b(HALF - 1, 0, 4)
            step_b(HALF - 1, 1, 5, ahead=False)

            for s in range(2):
                sp.wait_ge(x1_scattered[s], 64 * HALF)
                sp.wait_ge(added[s], 64 * HALF)

            def load_sums(g, slot):
                sp.dma_start(d_n[slot % RN][:, :], node_rows(sum_dram, g)).then_inc(f_sum_ld[slot % RN], 16)

            def load_x1(g, slot):
                sp.dma_start(d_x[slot][:, :], node_rows(x1_dram, g)).then_inc(f_x1_ld[slot], 16)

            def step_f(g, slot, more=True):
                if more or g + RN < NG:
                    sp.wait_ge(f_turned, QUADS * g + QUADS)
                    load_sums(g + RN, slot)
                if more or g + RX - 1 < NG:
                    load_x1(g + RX - 1, (slot - 1) % RX)
                sp.wait_ge(f_out, QUADS * g + QUADS)
                sp.dma_start(node_rows(out, g), d_x1[slot % RN][:, :]).then_inc(out_stored[slot % RN], 16)

            for g in range(RN):
                load_sums(g, g)
            for g in range(RX - 1):
                load_x1(g, g)
            with sp.Fori(0, ROUNDS) as m:
                for i in range(RX):
                    step_f(m * RX + i, i)
            for g in range(ROUNDS * RX, NG):
                if g == NG - 1:
                    sp.wait_ge(out_stored[(g - 1) % RN], 16 * in_slot[(g - 1) % RN])
                step_f(g, g % RX, more=False)
            for i in range(RN):
                sp.wait_ge(out_stored[i], 16 * in_slot[i])

        @block.gpsimd
        def _(pool):
            pool.memset(raw[:, 0, :], 0)
            pool.memset(raw[:, 1, :], SKIP)
            pool.memset(raw[:, 2:4, :], -1)
            pool.memset(weight_f[:, :], 0.0).then_inc(pads_set, 1)
            pool.memset(zero[:, :], 0.0).then_inc(zero_set, 1)
            pool.memset(lower[:, :], 0.0)
            pool.memset(ident[:, :], 0.0)
            pool.memset(ones3[:, :], 1.0).then_inc(zero_set, 1)
            pool.wait_ge(zero_set, 2)
            pool.affine_select(out=ident[:, :], in_=ident[:, :], compare_op=ALU.not_equal, fill=1.0, base=0,
                               pattern=[[-1, P]], channel_multiplier=1)
            pool.affine_select(out=lower[:, :].rearrange("p (j c) -> p j c", j=TILES),
                               in_=lower[:, :].rearrange("p (j c) -> p j c", j=TILES), compare_op=ALU.is_ge, fill=1.0, base=0,
                               pattern=[[0, TILES], [-1, P]], channel_multiplier=1)
            pool.iota(dump_i[:, :], pattern=[[P, TILES]], base=N, channel_multiplier=1).then_inc(pool_const, 1)

            pool.wait_ge(index_ready, 3)
            pool.wait_ge(store_setup, 96)

            def gathers(k, u, t0):
                s = u % 2
                pool.wait_ge(gidx_loaded[s], 16 * turn(k, u))
                if t0 >= 2:
                    pool.wait_ge(norm_src, 2 * k + u - 1)
                pool.sem_inc(pool_step, 1)
                for j in range(TILES):
                    pool.indirect_dma_start(a_xs[s][:, j * F:(j + 1) * F], None, x,
                                            bass.IndirectOffsetOnAxis(ap=gidx[s][:, j:j + 1], axis=0)).then_inc(src_gathered[s], 16)
                if t0 >= 2:
                    pool.wait_ge(base_ready, 2 * k + u - 1)
                    pool.sem_inc(pool_step, 1)
                for j in range(TILES):
                    pool.indirect_dma_start(a_xd[s][:, j * F:(j + 1) * F], None, x,
                                            bass.IndirectOffsetOnAxis(ap=gidx[s][:, 4 + j:5 + j], axis=0)).then_inc(dst_gathered[s], 16)

            for u in range(4):
                gathers(0, u, u)
            with pool.Fori(2, HALF) as k:
                for u in range(2):
                    gathers(k, u, 4)

            for i in range(RN):
                pool.wait_ge(x1_stored[i], 16 * in_slot[i])
            pool.wait_ge(cleared, 16 * NG)

            def scatters(k, u):
                s = u % 2
                pool.wait_ge(b_sidx_ld[s], 16 * turn(k, u))
                pool.wait_ge(b_x_ld[s], 16 * turn(k, u))
                pool.sem_inc(pool_step, 1)
                for j in range(TILES):
                    pool.indirect_dma_start(x1_dram, bass.IndirectOffsetOnAxis(ap=sidx[s][:, j:j + 1], axis=0),
                                            b_x[s][:, j * F:(j + 1) * F], None,
                                            bounds_check=bound, oob_is_err=False).then_inc(x1_scattered[s], 16)

            def adds(k, u, first=False):
                s = u % 2
                pool.wait_ge(b_at_ready, 2 * k + u + 1)
                pool.wait_ge(b_sum_ready, 2 * k + u + 1)
                if not first:
                    pool.wait_ge(added[1 - s], 64 * turn(k, u - 1))
                pool.sem_inc(pool_step, 1)
                for j in range(TILES):
                    pool.indirect_dma_start(sum_dram, bass.IndirectOffsetOnAxis(ap=b_at[s][:, j:j + 1], axis=0),
                                            b_sum[s][:, j * F:(j + 1) * F], None, compute_op=ALU.add).then_inc(added[s], 16)

            for u in range(4):
                scatters(0, u)
                if u >= 2:
                    adds(0, u - 2, first=u == 2)
            with pool.Fori(2, HALF) as k:
                for u in range(2):
                    scatters(k, u)
                    adds(k, u - 2)
            for u in range(2):
                adds(HALF, u - 2)

        def statistics(dve, st, n, six_done, sumdif_done, sq_done, var_done, at, count):
            dve.wait_ge(six_done, count)
            dve.tensor_tensor(st["sum"][:, 0:n], st["six"][:, 0:n, 1], st["six"][:, 0:n, 4], ALU.add)
            dve.tensor_tensor(st["sq"][:, 0:n], st["six"][:, 0:n, 2], st["six"][:, 0:n, 5], ALU.add)
            dve.tensor_tensor(st["dif"][:, 0:n], st["six"][:, 0:n, 1], st["six"][:, 0:n, 4], ALU.subtract).then_inc(sumdif_done, 1)
            dve.wait_ge(sumdif_done, count)
            dve.scalar_tensor_tensor(out=st["sq2"][:, 0:n], in0=st["dif"][:, 0:n], scalar=F / 4.0, in1=st["dif"][:, 0:n],
                                     op0=ALU.mult, op1=ALU.mult).then_inc(sq_done, 1)
            dve.wait_ge(sq_done, count)
            dve.tensor_tensor(st["var"][:, 0:n], st["sq"][:, 0:n], st["sq2"][:, 0:n], ALU.add).then_inc(var_done, 1)

        def inverse_deviation(act, st, n, var_done, log_done, rstd_done, count):
            act.wait_ge(var_done, count)
            act.activation(st["log"][:, 0:n], st["var"][:, 0:n], ACT.Ln, scale=1.0 / F, bias=EPS).then_inc(log_done, 1)
            act.wait_ge(log_done, count)
            act.activation(st["rstd"][:, 0:n], st["log"][:, 0:n], ACT.Exp, scale=-0.5).then_inc(rstd_done, 1)

        def shifts(dve, st, n, rstd_done, shift_done, count):
            dve.wait_ge(rstd_done, count)
            dve.scalar_tensor_tensor(out=st["shift"][:, 0:n], in0=st["sum"][:, 0:n], scalar=-0.5, in1=st["rstd"][:, 0:n],
                                     op0=ALU.mult, op1=ALU.mult).then_inc(shift_done, 1)

        ONE = slice(0, 1)

        @block.vector
        def _(dve):
            n_setup = [0]

            def link(ins):
                n_setup[0] += 1
                ins.then_inc(setup, 1)
                dve.wait_ge(setup, n_setup[0])

            dve.wait_ge(load_raw, 16 * N_RAW)
            dve.tensor_copy(rawf[:, :, :], raw[:, :, :]).then_inc(keep_ready, 1)
            dve.wait_ge(keep_ready, 1)
            dve.tensor_tensor(keep_b[:, :], rawf[:, 1, :], rawf[:, 3, :], ALU.is_equal).then_inc(keep_ready, 1)
            dve.tensor_scalar(gather_f[:, :], rawf[:, 1, :], float(N - 1), None, ALU.min)
            link(dve.tensor_tensor(goes_f[:, :], rawf[:, 1, :], rawf[:, 2, :], ALU.is_equal))
            dve.scalar_tensor_tensor(out=scatter_f[:, :], in0=goes_f[:, :], scalar=float(SKIP), in1=rawf[:, 1, :],
                                     op0=ALU.mult, op1=ALU.add).then_inc(index_f_ready, 1)
            dve.tensor_copy(goes_b[:, :], goes_f[:, :]).then_inc(keep_ready, 1)
            dve.memset(ones[:, :], 1.0)
            link(dve.memset(heads[:, :], 0.0))
            for h in range(HEADS):
                last = dve.memset(heads[h * HC:(h + 1) * HC, h * HC:(h + 1) * HC], 1.0)
            link(last)
            dve.wait_ge(load_const, 16 * N_CONST)
            dve.wait_ge(pool_const, 1)
            dve.tensor_scalar(neg_wl[:, :], wl[:, :], -1.0, None, ALU.mult)
            dve.tensor_tensor(wlr[:, :], wl[:, :], wr[:, :], ALU.add)
            dve.tensor_scalar(att_relu[:, :], heads[:, :], cols[:, 0:1], 1.0 - SLOPE, ALU.mult, ALU.mult)
            dve.tensor_scalar(neg_att_relu[:, :], heads[:, :], cols[:, 0:1], SLOPE - 1.0, ALU.mult, ALU.mult)
            dve.tensor_scalar(att_lin[:, :], heads[:, :], cols[:, 0:1], SLOPE, ALU.mult, ALU.mult)
            dve.tensor_tensor(cols[:, 3:4], cols[:, 1:2], cols[:, 2:3], ALU.add).then_inc(weights_ready, 1)
            for n in range(3):
                dve.tensor_copy(bo1_3[:, n:n + 1], cols[:, 5:6])
            dve.tensor_scalar(cols[:, 6:7], cols[:, 5:6], -1.0, None, ALU.mult).then_inc(bo1_ready, 1)
            dve.wait_ge(index_turned, 4)
            dve.tensor_tensor(part3[:, 0, F:2 * F], rows3[:, 2 * F:3 * F], bank[3][0:3, 0:F], ALU.add)
            link(dve.tensor_tensor(part3[:, 0, 0:F], rows3[:, 0:F], rows3[:, F:2 * F], ALU.add))
            link(dve.tensor_copy(part3b[:, 0, :], part3[:, 0, :]))
            link(dve.tensor_tensor(part3[:, 1, :], part3[:, 0, :], part3b[:, 0, :], ALU.subtract))
            link(dve.tensor_copy(part3b[:, 1, :], part3[:, 1, :]))
            link(dve.tensor_tensor(part3[:, 2, :], part3[:, 1, :], part3b[:, 1, :], ALU.subtract))
            link(dve.tensor_scalar(sel3[:, 0, :], part3b[:, 0, :], ident[0:3, 0:1], None, ALU.mult))
            link(dve.scalar_tensor_tensor(out=sel3[:, 1, :], in0=part3b[:, 1, :], scalar=ident[0:3, 1:2], in1=sel3[:, 0, :],
                                          op0=ALU.mult, op1=ALU.add))
            link(dve.scalar_tensor_tensor(out=sel3[:, 0, :], in0=part3[:, 2, :], scalar=ident[0:3, 2:3], in1=sel3[:, 1, :],
                                          op0=ALU.mult, op1=ALU.add))
            for j in range(4):
                dve.tensor_copy(bias3[:, j, :], sel3[:, 0, 0:F])
                last = dve.tensor_copy(bo23[:, j, :], sel3[:, 0, F:2 * F])
            last.then_inc(parts, 1)
            dve.wait_ge(index_turned, 3)
            for i in range(3):
                dve.tensor_copy(index[:, :].rearrange("p (c i) -> p c i", i=12)[:, :, 4 * i:4 * i + 4],
                                bank[i][:, 0:4 * NC].rearrange("p (j c) -> p c j", j=4)).then_inc(index_ready, 1)
            dve.wait_ge(index_ready, 3)
            dve.tensor_copy(dump[:, :], dump_i[:, :])
            link(dve.tensor_copy(columns[:, :].rearrange("p (c i) -> p c i", i=8)[:, :, 0:4],
                                 index[:, :].rearrange("p (c i) -> p c i", i=12)[:, :, 0:4]))
            for j in range(TILES):
                last = dve.tensor_scalar(columns[:, :].rearrange("p (c i) -> p i c", i=8)[:, 4 + j, :],
                                         columns[:, :].rearrange("p (c i) -> p i c", i=8)[:, j, :],
                                         -1.0, dump[:, j:j + 1], ALU.mult, ALU.add)
            last.then_inc(columns_ready, 1)

            def sums_d(g, slot, m, half):
                if half == 0:
                    dve.wait_ge(xd_loaded[slot], 16 * (m + 1))
                for j in range(half * J // 2, (half + 1) * J // 2):
                    last = dve.bn_stats(stat_d[slot % 2]["six"][:, j, :], d_x[slot][:, j * F:(j + 1) * F])
                if half:
                    last.then_inc(d_six, 1)

            def x1_d(g, slot, m, q):
                dve.wait_ge(d_mm, QUADS * g + q + 1)
                if q == 0 and not (isinstance(g, int) and g < RN):
                    dve.wait_ge(x1_stored[slot % RN], 16 * (RX // RN * m + slot // RN))
                dve.tensor_tensor(d_x1[slot % RN][:, q * 512:(q + 1) * 512], bank[2 + q % 2][:, :],
                                  d_x[slot][:, q * 512:(q + 1) * 512], ALU.add).then_inc(d_x1_ready, 1)

            def statistics_d(g, slot):
                if not (isinstance(g, int) and g < 2):
                    dve.wait_ge(d_norm_act, QUADS * (g - 1))
                    dve.wait_ge(d_norm_dve, g - 1)
                statistics(dve, stat_d[slot % 2], J, d_six, d_sumdif, d_sq, d_var, g, g + 1)

            def step_d(g, slot, m, front=True, back=True, back2=True, ahead=True):
                before = ((slot - 1) % RX, m if slot else m - 1)
                before2 = ((slot - 2) % RX, m if slot > 1 else m - 1)
                after = ((slot + 1) % RX, m if slot < RX - 1 else m + 1)
                if front:
                    st = stat_d[slot % 2]
                    shifts(dve, st, J, d_rstd, d_shift, g + 1)
                if back2:
                    x1_d(g - 2, *before2, 3)
                if front:
                    dve.wait_ge(d_shift, g + 1)
                    if not (isinstance(g, int) and g < RN):
                        dve.wait_ge(d_turned, QUADS * (g - 1))
                    for j in range(J_ACT, J):
                        last = dve.tensor_scalar(d_n[slot % RN][:, j * F:(j + 1) * F], d_x[slot][:, j * F:(j + 1) * F],
                                                 st["rstd"][:, j:j + 1], st["shift"][:, j:j + 1], ALU.mult, ALU.add)
                    last.then_inc(d_norm_dve, 1)
                if ahead:
                    sums_d(g + 1, *after, 0)
                if back:
                    x1_d(g - 1, *before, 0)
                if ahead:
                    sums_d(g + 1, *after, 1)
                if back:
                    x1_d(g - 1, *before, 1)
                if ahead:
                    statistics_d(g + 1, after[0])
                if back:
                    x1_d(g - 1, *before, 2)

            sums_d(0, 0, 0, 0)
            sums_d(0, 0, 0, 1)
            statistics_d(0, 0)
            for g in range(RX):
                step_d(g, g, 0, back=g > 0, back2=g > 1)
            with dve.Fori(1, 1 + ROUNDS) as m:
                for i in range(RX):
                    step_d(m * RX + i, i, m)
            for g in range((1 + ROUNDS) * RX, NG + 1):
                step_d(g, g % RX, g // RX, front=g < NG, ahead=g < NG - 1)
            x1_d(NG - 1, (NG - 1) % RX, (NG - 1) // RX, 3)

            def sums_a(k, u):
                s = u % 2
                st = stat_e[s]
                dve.wait_ge(src_gathered[s], 64 * turn(k, u))
                for j in range(TILES):
                    dve.bn_stats(st["six"][:, j, :], a_xs[s][:, j * F:(j + 1) * F])
                dve.wait_ge(dst_gathered[s], 64 * turn(k, u))
                for j in range(TILES):
                    last = dve.bn_stats(st["six"][:, TILES + j, :], a_xd[s][:, j * F:(j + 1) * F])
                last.then_inc(six, 1)

            def norms_a(k, u, t0):
                s = u % 2
                t = 2 * k + u
                st = stat_e[s]
                if t0 >= 1:
                    dve.wait_ge(turned_dst, t)
                dve.wait_ge(shift, t + 1)
                for j in range(DST_ACT, TILES):
                    last = dve.tensor_scalar(a_nd[:, j * F:(j + 1) * F], a_xd[s][:, j * F:(j + 1) * F],
                                             st["rstd"][:, TILES + j:TILES + j + 1], st["shift"][:, TILES + j:TILES + j + 1],
                                             ALU.mult, ALU.add)
                last.then_inc(norm_dst, 1)

            def step_a(k, u, t0, ahead=True, front=True, mid=True, back=True):
                s = u % 2
                t = 2 * k + u
                o = 1 - s
                if mid:
                    dve.wait_ge(score_mm, t)
                    dve.wait_ge(keep_loaded[o], 16 * turn(k, u - 1))
                    if t0 == 1:
                        dve.memset(a_max[o][:, 0:1], 0.0).then_inc(max_carry, 1)
                        first = 0.0
                    else:
                        dve.tensor_copy(a_max[o][:, 0:1], a_max[s][:, C:C + 1]).then_inc(max_carry, 1)
                        first = a_max[s][:, C:C + 1]
                    dve.tensor_tensor_scan(a_max[o][:, 1:C + 1], a_keep[o][:, :], bank[5][:, :], first,
                                           ALU.mult, ALU.max).then_inc(max_scan, 1)
                    dve.wait_ge(max_carry, t)
                    dve.wait_ge(max_scan, t)
                    dve.tensor_tensor(a_d1[:, :], a_max[o][:, 0:C], a_max[o][:, 1:C + 1], ALU.subtract).then_inc(dif_decay, 1)
                    dve.tensor_tensor(a_d2[:, :], bank[5][:, :], a_max[o][:, 1:C + 1], ALU.subtract).then_inc(dif_score, 1)
                if back:
                    dve.wait_ge(out_turned, t - 1)
                    if t0 >= 4:
                        dve.wait_ge(end_stored[s], 16 * turn(k, u - 4))
                    dve.tensor_tensor(a_x1[s][:, :], bank[7][:, :], a_base[s][:, :], ALU.add).then_inc(x1_ready, 1)
                if ahead:
                    sums_a(k, u + 1)
                if front:
                    dve.wait_ge(base_mm, t + 1)
                    if back:
                        dve.wait_ge(x1_ready, t - 1)
                    dve.tensor_tensor(a_base[s][:, :], bank[6][:, :], a_xd[s][:, :], ALU.add).then_inc(base_ready, 1)
                if ahead:
                    statistics(dve, stat_e[o], 2 * TILES, six, sumdif, sq, var, t + 1, t + 2)
                if mid:
                    dve.wait_ge(exp_decay, t)
                    dve.scalar_tensor_tensor(out=a_dec[:, :], in0=a_decay[:, :], scalar=1.0, in1=a_keep[o][:, :],
                                             op0=ALU.min, op1=ALU.mult).then_inc(decay, 1)
                if ahead:
                    shifts(dve, stat_e[o], 2 * TILES, rstd, shift, t + 2)
                if mid:
                    dve.wait_ge(exp_score, t)
                    dve.wait_ge(decay, t)
                    dve.tensor_tensor_scan(a_den[o][:, :], a_dec[:, :], a_p[:, :], 0.0 if t0 == 1 else a_den[s][:, C - 1:C],
                                           ALU.mult, ALU.add).then_inc(den_scan, 1)
                    dve.tensor_tensor(a_pv[:, :], a_p[:, :], a_v[o][:, :], ALU.mult).then_inc(weighted, 1)
                    dve.wait_ge(den_scan, t)
                    dve.wait_ge(exp_self, t)
                    dve.tensor_tensor(a_all[:, :], a_den[o][:, :], a_ps[:, :], ALU.add).then_inc(den_all, 1)
                if mid:
                    dve.wait_ge(weighted, t)
                    dve.tensor_tensor_scan(a_sum[o][:, :], a_dec[:, :], a_pv[:, :], 0.0 if t0 == 1 else a_sum[s][:, C - 1:C],
                                           ALU.mult, ALU.add).then_inc(sum_scan, 1)
                if ahead:
                    norms_a(k, u + 1, t0 + 1)
                if mid:
                    dve.wait_ge(den_rec, t)
                    dve.wait_ge(sum_scan, t)
                    dve.tensor_tensor(a_o[o][:, :], a_sum[o][:, :], a_rec[:, :], ALU.mult).then_inc(att_out, 1)

            sums_a(0, 0)
            statistics(dve, stat_e[0], 2 * TILES, six, sumdif, sq, var, 0, 1)
            shifts(dve, stat_e[0], 2 * TILES, rstd, shift, 1)
            norms_a(0, 0, 0)
            for u in range(4):
                step_a(0, u, u, mid=u >= 1, back=u >= 2)
            with dve.Fori(2, HALF - 1) as k:
                for u in range(2):
                    step_a(k, u, 4 + u)
            step_a(HALF - 1, 0, 4)
            step_a(HALF - 1, 1, 5, ahead=False)
            step_a(HALF, 0, 4, ahead=False, front=False)
            step_a(HALF, 1, 5, ahead=False, front=False, mid=False)

            for s in range(2):
                dve.wait_ge(end_stored[s], 16 * HALF)
            dve.memset(b_f[:, :], 1.0).then_inc(ones_set, 1)

            def sums_b(k, u):
                s = u % 2
                dve.wait_ge(b_x_ld[s], 16 * turn(k, u))
                for j in range(TILES):
                    last = dve.bn_stats(stat_e[s]["six"][:, j, :], b_x[s][:, j * F:(j + 1) * F])
                last.then_inc(b_six, 1)
                statistics(dve, stat_e[s], TILES, b_six, b_sumdif, b_sq, b_var, 2 * k + u, 2 * k + u + 1)

            def step_b(k, u, t0, ahead=True, front=True, mid=True, back=True):
                s = u % 2
                o = 1 - s
                t = 2 * k + u
                if mid:
                    dve.wait_ge(b_hf, t)
                    dve.wait_ge(b_goes_ld[o], 16 * turn(k, u - 1))
                    dve.scalar_tensor_tensor(out=b_neg[:, :], in0=b_goes[o][:, :], scalar=1.0, in1=bank[3][:, :],
                                             op0=ALU.subtract, op1=ALU.mult).then_inc(b_neg_ready, 1)
                    dve.wait_ge(b_filter, t)
                    dve.wait_ge(b_w_ld[o], 16 * turn(k, u - 1))
                    dve.scalar_tensor_tensor(out=b_t[:, :], in0=bank[4][:, :], scalar=cols[:, 4:5], in1=b_w[o][:, :],
                                             op0=ALU.add, op1=ALU.mult).then_inc(b_t_ready, 1)
                    dve.wait_ge(b_neg_ready, t)
                    dve.tensor_tensor_scan(b_fill[o][:, ::-1], b_goes[o][:, ::-1], b_neg[:, ::-1],
                                           0.0 if t0 == 1 else b_fill[s][:, 0:1], ALU.mult, ALU.subtract).then_inc(b_fill_ready, 1)
                    dve.wait_ge(b_fill_ready, t)
                    dve.wait_ge(b_t_ready, t)
                    if t0 >= 2:
                        dve.wait_ge(b_msg_turned, t - 1)
                    dve.tensor_tensor(b_msg[:, :], b_fill[o][:, :], b_t[:, :], ALU.mult).then_inc(b_msg_ready, 1)
                if ahead:
                    sums_b(k, u + 1)
                if front:
                    dve.wait_ge(b_ln_done, t + 1)
                    dve.scalar_tensor_tensor(out=b_s1[:, :], in0=bank[1][:, :], scalar=0.0, in1=b_ln[:, :],
                                             op0=ALU.max, op1=ALU.add).then_inc(b_s1_ready, 1)
                if mid:
                    dve.wait_ge(b_part1, t)
                    dve.tensor_tensor(b_rest[:, :], bank[5][:, :], b_rows[o][:, 0, :], ALU.subtract).then_inc(b_rest1, 1)
                if ahead:
                    shifts(dve, stat_e[o], TILES, b_rstd, b_shift, t + 2)
                if back:
                    dve.wait_ge(b_count, t - 1)
                    dve.scalar_tensor_tensor(out=b_dup[:, :], in0=bank[7][:, 0:TILES], scalar=1.0, in1=b_col[s][:, TILES:2 * TILES],
                                             op0=ALU.min, op1=ALU.mult).then_inc(b_dup_ready, 1)
                    dve.wait_ge(b_dup_ready, t - 1)
                    if t0 >= 4:
                        dve.wait_ge(added[s], 64 * turn(k, u - 4))
                    dve.tensor_tensor(b_at[s][:, :], b_dup[:, :], b_col[s][:, 0:TILES], ALU.add).then_inc(b_at_ready, 1)
                if mid:
                    dve.wait_ge(b_src_ld[o], 16 * turn(k, u - 1))
                    dve.wait_ge(b_col_ld[o], 16 * turn(k, u - 1))
                    if t0 >= 3:
                        dve.wait_ge(b_summed, t - 2)
                    for j in range(TILES):
                        last = dve.tensor_scalar(b_same[o][:, j, :], b_src[o][:, :], b_col[o][:, j:j + 1], None, ALU.is_equal)
                    last.then_inc(b_same_ready, 1)
                    dve.wait_ge(b_part2, t)
                    dve.tensor_tensor(b_rows[o][:, 2, :], b_rest[:, :], b_rows[o][:, 1, :], ALU.subtract).then_inc(b_part3, 1)
                    dve.wait_ge(b_same_ready, t)
                    if t0 >= 2:
                        dve.wait_ge(b_count, t - 1)
                    own = b_same[o][:, :, :]
                    own = bass.AP(tensor=own.tensor, offset=own.offset, ap=[list(own.ap[0]), [C + P, TILES], [1, P]])
                    dve.tensor_tensor(b_before[:, :].rearrange("p (j c) -> p j c", j=TILES), own,
                                      lower[:, :].rearrange("p (j c) -> p j c", j=TILES), ALU.mult).then_inc(b_before_ready, 1)

            sums_b(0, 0)
            shifts(dve, stat_e[0], TILES, b_rstd, b_shift, 1)
            for u in range(4):
                step_b(0, u, u, mid=u >= 1, back=u >= 2)
            with dve.Fori(2, HALF - 1) as k:
                for u in range(2):
                    step_b(k, u, 4 + u)
            step_b(HALF - 1, 0, 4)
            step_b(HALF - 1, 1, 5, ahead=False)
            step_b(HALF, 0, 4, ahead=False, front=False)
            step_b(HALF, 1, 5, ahead=False, front=False, mid=False)

            def f_ssp(c, q, c0):
                dve.wait_ge(f_ln, c + 1)
                if c0 >= 2:
                    dve.wait_ge(f_y, c - 1)
                dve.scalar_tensor_tensor(out=f_ssp_out[q % 2][:, :], in0=bank[2 + q % 2][:, :], scalar=cols[:, 6:7],
                                         in1=f_ln_out[q % 2][:, :], op0=ALU.max, op1=ALU.add).then_inc(f_s, 1)

            def f_rows(c, q, slot, m, c0):
                dve.wait_ge(f_y, c + 1)
                if q == 0:
                    dve.wait_ge(f_x1_ld[slot], 16 * (m + 1))
                    if c0 >= QUADS * RN:
                        dve.wait_ge(out_stored[slot % RN], 16 * (RX // RN * m + slot // RN))
                dve.tensor_tensor(d_x1[slot % RN][:, q * 512:(q + 1) * 512], bank[4 + q % 2][:, :],
                                  d_x[slot][:, q * 512:(q + 1) * 512], ALU.add).then_inc(f_out, 1)

            def f_group(g, slot, m, g0):
                for q in range(QUADS):
                    f_ssp(QUADS * g + q, q, QUADS * g0 + q)
                    if q >= 2:
                        f_rows(QUADS * g + q - 2, q - 2, slot, m, QUADS * g0 + q - 2)
                    elif g0:
                        f_rows(QUADS * g + q - 2, QUADS + q - 2, (slot - 1) % RX, m if slot else m - 1, QUADS * g0 + q - 2)

            for g in range(RX):
                f_group(g, g, 0, g)
            with dve.Fori(1, 1 + ROUNDS) as m:
                for i in range(RX):
                    f_group(m * RX + i, i, m, RX)
            for g in range((1 + ROUNDS) * RX, NG):
                f_group(g, g % RX, g // RX, g)
            for n in (2, 1):
                f_rows(QUADS * NG - n, QUADS - n, (NG - 1) % RX, (NG - 1) // RX, QUADS * NG - n)

        @block.scalar
        def _(act):
            act.preload_act_table_set("natural_log_exp_and_others")
            def step_d(g, slot, front=True, back=True, ahead=True):
                if front:
                    act.wait_ge(d_shift, g + 1)
                    if not (isinstance(g, int) and g < RN):
                        act.wait_ge(d_turned, QUADS * (g - 1))
                for q in range(QUADS):
                    if back:
                        c = QUADS * (g - 1) + q
                        act.wait_ge(d_turned, c + 1)
                        if not (isinstance(c, int) and c < 2):
                            act.wait_ge(d_mm, c - 1)
                        act.activation(turned[q % 2][:, :], bank[q % 2][:, :], ACT.Relu).then_inc(d_relu, 1)
                    if front:
                        for j in range(4 * q, min(4 * q + 4, J_ACT)):
                            last = act.activation(d_n[slot % RN][:, j * F:(j + 1) * F], d_x[slot][:, j * F:(j + 1) * F], ACT.Relu,
                                                  scale=stat_d[slot % 2]["rstd"][:, j:j + 1], bias=stat_d[slot % 2]["shift"][:, j:j + 1])
                        last.then_inc(d_norm_act, 1)
                if ahead:
                    if not (isinstance(g, int) and g < 1):
                        act.wait_ge(d_norm_dve, g)
                    inverse_deviation(act, stat_d[(slot + 1) % 2], J, d_var, d_log, d_rstd, g + 2)

            inverse_deviation(act, stat_d[0], J, d_var, d_log, d_rstd, 1)
            for g in range(RX):
                step_d(g, g, back=g > 0)
            with act.Fori(1, 1 + ROUNDS) as m:
                for i in range(RX):
                    step_d(m * RX + i, i)
            for g in range((1 + ROUNDS) * RX, NG + 1):
                step_d(g, g % RX, front=g < NG, ahead=g < NG - 1)

            def norm_tile(to, rows, st, n, j):
                return act.activation(to[:, j * F:(j + 1) * F], rows[:, j * F:(j + 1) * F], ACT.Relu,
                                      scale=st["rstd"][:, n:n + 1], bias=st["shift"][:, n:n + 1])

            def norms_dst(k, u, t0):
                s = u % 2
                t = 2 * k + u
                act.wait_ge(shift, t + 1)
                if t0 >= 1:
                    act.wait_ge(turned_dst, t)
                for j in range(DST_ACT):
                    norm_tile(a_nd, a_xd[s], stat_e[s], TILES + j, j)

            def norms_src(k, u):
                s = u % 2
                for j in range(TILES):
                    last = norm_tile(a_ns, a_xs[s], stat_e[s], j, j)
                last.then_inc(norm_src, 1)

            def step_a(k, u, t0, ahead=True, front=True, mid=True):
                s = u % 2
                o = 1 - s
                t = 2 * k + u
                if front:
                    act.wait_ge(turned_src, t + 1)
                    if t0 >= 1:
                        act.wait_ge(edge_mm, t)
                    act.activation(a_hs[:, :], bank[0][:, :], ACT.Copy)
                    act.wait_ge(turned_dst, t + 1)
                    act.activation(a_hd[:, :], bank[1][:, :], ACT.Relu).then_inc(h_dst, 1)
                if mid:
                    act.wait_ge(dif_decay, t)
                    act.activation(a_decay[:, :], a_d1[:, :], ACT.Exp).then_inc(exp_decay, 1)
                    act.wait_ge(dif_score, t)
                    act.activation(a_p[:, :], a_d2[:, :], ACT.Exp).then_inc(exp_score, 1)
                    act.activation(a_ps[:, :], a_max[o][:, 1:C + 1], ACT.Exp, scale=-1.0).then_inc(exp_self, 1)
                if front:
                    act.wait_ge(self_mm, t + 1)
                    if t0 >= 1:
                        act.wait_ge(score_mm, t)
                    act.activation(a_us[:, :], bank[2][:, :], ACT.Relu, bias=cols[:, 3:4]).then_inc(self_relu, 1)
                if ahead:
                    inverse_deviation(act, stat_e[o], 2 * TILES, var, log_var, rstd, t + 2)
                if front:
                    act.wait_ge(v_mm, t + 1)
                    act.activation(a_v[s][:, :], bank[3][:, :], ACT.Copy).then_inc(v_copied, 1)
                if ahead:
                    norms_dst(k, u + 1, t0 + 1)
                if ahead:
                    norms_src(k, u + 1)
                if front:
                    act.wait_ge(edge_mm, t + 1)
                    act.activation(a_u[:, :], bank[4][:, :], ACT.Relu, bias=cols[:, 3:4]).then_inc(edge_relu, 1)
                if mid:
                    act.wait_ge(den_all, t)
                    act.activation(a_log[:, :], a_all[:, :], ACT.Ln).then_inc(den_log, 1)
                    act.wait_ge(den_log, t)
                    act.activation(a_rec[:, :], a_log[:, :], ACT.Exp, scale=-1.0).then_inc(den_rec, 1)

            act.wait_ge(weights_ready, 1)
            inverse_deviation(act, stat_e[0], 2 * TILES, var, log_var, rstd, 1)
            norms_dst(0, 0, 0)
            norms_src(0, 0)
            for u in range(4):
                step_a(0, u, u, mid=u >= 1)
            with act.Fori(2, HALF - 1) as k:
                for u in range(2):
                    step_a(k, u, 4 + u)
            step_a(HALF - 1, 0, 4)
            step_a(HALF - 1, 1, 5, ahead=False)
            step_a(HALF, 0, 4, ahead=False, front=False)

            def softplus(z, ab, ex, ln, z_done, abs_done, exp_done, ln_done, count, bias=0.0, between=lambda: None):
                act.wait_ge(z_done, count)
                act.activation(ab[:, :], z[:, :], ACT.Abs, bias=bias).then_inc(abs_done, 1)
                between()
                act.wait_ge(abs_done, count)
                act.activation(ex[:, :], ab[:, :], ACT.Exp, scale=-1.0).then_inc(exp_done, 1)
                act.wait_ge(exp_done, count)
                act.activation(ln[:, :], ex[:, :], ACT.Ln, scale=0.5, bias=0.5).then_inc(ln_done, 1)

            def norms_b(k, u, t0):
                s = u % 2
                t = 2 * k + u
                st = stat_e[s]
                act.wait_ge(b_shift, t + 1)
                if t0 >= 1:
                    act.wait_ge(b_turned, t)
                for j in range(TILES):
                    last = act.activation(b_n[:, j * F:(j + 1) * F], b_x[s][:, j * F:(j + 1) * F], ACT.Relu,
                                          scale=st["rstd"][:, j:j + 1], bias=st["shift"][:, j:j + 1])
                last.then_inc(b_norm, 1)

            def step_b(k, u, t0, ahead=True, front=True, mid=True, back=True):
                s = u % 2
                o = 1 - s
                t = 2 * k + u
                if front:
                    act.wait_ge(b_fa_turned, t + 1)
                    act.activation(b_f[0:RBF, :].rearrange("r (p j) -> r j p", j=TILES),
                                   bank[0][0:RBF, :].rearrange("r (j p) -> r j p", j=TILES), ACT.Copy).then_inc(b_f_ready, 1)
                    act.wait_ge(b_turned, t + 1)
                    if t0 >= 1:
                        act.wait_ge(b_hf, t)
                    act.activation(b_h[:, :], bank[2][:, :], ACT.Copy).then_inc(b_h_ready, 1)
                    if t0 >= 1:
                        act.wait_ge(b_s1_ready, t)
                    softplus(bank[1], b_abs, b_exp, b_ln, b_z1, b_abs_done, b_exp_done, b_ln_done, t + 1)
                if mid:
                    act.wait_ge(b_msg_turned, t)
                    if t0 >= 3:
                        act.wait_ge(b_summed, t - 2)
                    act.activation(b_rows[o][:, 0, :], bank[5][:, :], ACT.Copy).then_inc(b_part1, 1)
                if ahead:
                    inverse_deviation(act, stat_e[o], TILES, b_var, b_logv, b_rstd, t + 2)
                if mid:
                    act.wait_ge(b_rest1, t)
                    act.activation(b_rows[o][:, 1, :], b_rest[:, :], ACT.Copy).then_inc(b_part2, 1)
                if back:
                    act.wait_ge(b_summed, t - 1)
                    if t0 >= 4:
                        act.wait_ge(added[s], 64 * turn(k, u - 4))
                    act.activation(b_sum[s][:, :], bank[6][:, :], ACT.Copy).then_inc(b_sum_ready, 1)
                if ahead:
                    norms_b(k, u + 1, t0 + 1)

            act.wait_ge(ones_set, 1)
            inverse_deviation(act, stat_e[0], TILES, b_var, b_logv, b_rstd, 1)
            norms_b(0, 0, 0)
            for u in range(4):
                step_b(0, u, u, mid=u >= 1, back=u >= 2)
            with act.Fori(2, HALF - 1) as k:
                for u in range(2):
                    step_b(k, u, 4 + u)
            step_b(HALF - 1, 0, 4)
            step_b(HALF - 1, 1, 5, ahead=False)
            step_b(HALF, 0, 4, ahead=False, front=False)
            step_b(HALF, 1, 5, ahead=False, front=False, mid=False)

            def f_copy(c, q, c0):
                act.wait_ge(f_turned, c + 1)
                if c0 >= 2:
                    act.wait_ge(f_z, c - 1)
                act.activation(turned[q % 2][:, :], bank[q % 2][:, :], ACT.Copy).then_inc(f_copied, 1)

            def f_network(c, q, c0, between=lambda: None):
                if c0 >= 2:
                    act.wait_ge(f_s, c - 1)
                softplus(bank[2 + q % 2], f_abs_out, f_exp_out, f_ln_out[q % 2], f_z, f_abs, f_exp, f_ln, c + 1,
                         bias=cols[:, 5:6], between=between)

            def f_group(g, g0):
                for q in range(QUADS):
                    def copy():
                        f_copy(QUADS * g + q, q, QUADS * g0 + q)

                    if g0 or q:
                        f_network(QUADS * g + q - 1, q - 1, QUADS * g0 + q - 1, between=copy)
                    else:
                        copy()

            f_group(0, 0)
            with act.Fori(1, NG) as g:
                f_group(g, 1)
            f_network(QUADS * NG - 1, QUADS - 1, QUADS * NG - 1)

        @block.tensor
        def _(pe):
            def turn_tiles(to, tiles, n=TILES, width=F):
                for j in range(n):
                    last = pe.transpose(to[0:width, j * P:(j + 1) * P], tiles[:, j * width:(j + 1) * width], ident[:, :])
                return last

            pe.wait_ge(pool_const, 1)
            pe.wait_ge(index_f_ready, 1)
            for i, a in enumerate((rawf[:, 0, :], gather_f[:, :], scatter_f[:, :])):
                for j in range(TILES):
                    last = pe.transpose(bank[i][:, j * NC:(j + 1) * NC], a[0:NC, j * P:(j + 1) * P], ident[0:NC, 0:NC])
                last.then_inc(index_turned, 1)
            pe.wait_ge(load_const, 16 * N_CONST)
            pe.wait_ge(bo1_ready, 1)
            pe.matmul(bank[3][0:3, 0:F], bo1_3[:, :], wo2[:, :], start=True, stop=True).then_inc(index_turned, 1)
            pe.wait_ge(parts, 1)
            pe.wait_ge(index_ready, 3)

            def d_turn(g, slot, q):
                c = QUADS * g + q
                pe.wait_ge(d_norm_act, QUADS * g + q + 1)
                if q == QUADS - 1:
                    pe.wait_ge(d_norm_dve, g + 1)
                if not (isinstance(c, int) and c < 2):
                    pe.wait_ge(d_relu, c - 1)
                turn_tiles(bank[q % 2], d_n[slot % RN][:, q * 512:(q + 1) * 512]).then_inc(d_turned, 1)

            def d_multiply(g, q):
                c = QUADS * g + q
                to = bank[2 + q % 2]
                if not (isinstance(c, int) and c < 2):
                    pe.wait_ge(d_x1_ready, c - 1)
                pe.matmul(to[:, :], ones3[:, 0:P], bias3[:, :, :].rearrange("k j f -> k (j f)"), start=True, stop=False)
                pe.wait_ge(d_relu, c + 1)
                for j in range(4):
                    last = pe.matmul(to[:, j * F:(j + 1) * F], turned[q % 2][:, j * P:(j + 1) * P], wl[:, :],
                                     start=False, stop=(j == 3))
                last.then_inc(d_mm, 1)

            def step_d(g, slot):
                d_turn(g, slot, 0)
                for q in range(1, QUADS):
                    d_turn(g, slot, q)
                    d_multiply(g, q - 1)
                d_multiply(g, QUADS - 1)

            for g in range(RX):
                step_d(g, g)
            with pe.Fori(1, 1 + ROUNDS) as m:
                for i in range(RX):
                    step_d(m * RX + i, i)
            for g in range((1 + ROUNDS) * RX, NG):
                step_d(g, g % RX)

            pe.wait_ge(weights_ready, 1)

            def turn_a(t):
                pe.wait_ge(norm_src, t + 1)
                turn_tiles(bank[0], a_ns).then_inc(turned_src, 1)

            def step_a(k, u, t0, ahead=True, front=True, back=True):
                s = u % 2
                t = 2 * k + u
                if front:
                    pe.wait_ge(norm_dst, t + 1)
                    turn_tiles(bank[1], a_nd).then_inc(turned_dst, 1)
                if back:
                    pe.wait_ge(att_out, t - 1)
                    if t0 >= 3:
                        pe.wait_ge(x1_ready, t - 2)
                    turn_tiles(bank[7], a_o[s]).then_inc(out_turned, 1)
                if front:
                    if t0 >= 1:
                        pe.wait_ge(base_ready, t)
                    pe.matmul(bank[6][:, :], ones3[:, 0:P], bias3[:, :, :].rearrange("k j f -> k (j f)"), start=True, stop=False)
                    pe.wait_ge(h_dst, t + 1)
                    for j in range(TILES):
                        last = pe.matmul(bank[6][:, j * F:(j + 1) * F], a_hd[:, j * P:(j + 1) * P], wl[:, :],
                                         start=False, stop=(j == TILES - 1))
                    last.then_inc(base_mm, 1)
                    if t0 >= 1:
                        pe.wait_ge(edge_relu, t)
                    pe.matmul(bank[2][:, :], wlr[:, :], a_hd[:, :], start=True, stop=True).then_inc(self_mm, 1)
                    pe.matmul(bank[3][:, :], neg_wl[:, :], a_hd[:, :], start=True, stop=False)
                    pe.matmul(bank[3][:, :], wl[:, :], a_hs[:, :], start=False, stop=True).then_inc(v_mm, 1)
                    pe.matmul(bank[4][:, :], wl[:, :], a_hs[:, :], start=True, stop=False)
                    pe.matmul(bank[4][:, :], wr[:, :], a_hd[:, :], start=False, stop=True).then_inc(edge_mm, 1)
                    if t0 >= 1:
                        pe.wait_ge(dif_score, t)
                    pe.wait_ge(self_relu, t + 1)
                    pe.matmul(bank[5][:, :], neg_att_relu[:, :], a_us[:, :], start=True, stop=False)
                    pe.wait_ge(v_copied, t + 1)
                    pe.matmul(bank[5][:, :], att_lin[:, :], a_v[s][:, :], start=False, stop=False)
                if ahead:
                    turn_a(t + 1)
                if front:
                    pe.wait_ge(edge_relu, t + 1)
                    pe.matmul(bank[5][:, :], att_relu[:, :], a_u[:, :], start=False, stop=True).then_inc(score_mm, 1)

            turn_a(0)
            for u in range(4):
                step_a(0, u, u, back=u >= 2)
            with pe.Fori(2, HALF - 1) as k:
                for u in range(2):
                    step_a(k, u, 4 + u)
            step_a(HALF - 1, 0, 4)
            step_a(HALF - 1, 1, 5, ahead=False)
            for u in range(2):
                step_a(HALF, u, 4 + u, ahead=False, front=False)

            def step_b(k, u, t0, front=True, mid=True, back=True):
                s = u % 2
                t = 2 * k + u
                if front:
                    pe.wait_ge(b_fa_ld[s], 16 * turn(k, u))
                    if t0 >= 1:
                        pe.wait_ge(b_f_ready, t)
                    turn_tiles(bank[0], b_fa[s], width=RBF).then_inc(b_fa_turned, 1)
                    pe.wait_ge(b_norm, t + 1)
                    if t0 >= 1:
                        pe.wait_ge(b_h_ready, t)
                    turn_tiles(bank[2], b_n).then_inc(b_turned, 1)
                    pe.wait_ge(b_f_ready, t + 1)
                    if t0 >= 1:
                        pe.wait_ge(b_s1_ready, t)
                    pe.matmul(bank[1][:, :], wf1[0:RBF + 1, :], b_f[0:RBF + 1, :], start=True, stop=True).then_inc(b_z1, 1)
                    pe.wait_ge(b_h_ready, t + 1)
                    if t0 >= 1:
                        pe.wait_ge(b_neg_ready, t)
                    pe.matmul(bank[3][:, :], win[:, :], b_h[:, :], start=True, stop=True).then_inc(b_hf, 1)
                if mid:
                    pe.wait_ge(b_msg_ready, t)
                    if t0 >= 2:
                        pe.wait_ge(b_rest1, t - 1)
                    turn_tiles(bank[5], b_msg).then_inc(b_msg_turned, 1)
                if back:
                    pe.wait_ge(b_before_ready, t - 1)
                    if t0 >= 3:
                        pe.wait_ge(b_dup_ready, t - 2)
                    for i in range(TILES):
                        for j in range(i):
                            pe.matmul(bank[7][:, i:i + 1], b_same[s][:, j, i * P:(i + 1) * P], ones[:, 0:1], start=(j == 0), stop=False)
                        last = pe.matmul(bank[7][:, i:i + 1], b_before[:, i * P:(i + 1) * P], ones[:, 0:1], start=(i == 0), stop=True)
                    last.then_inc(b_count, 1)
                    pe.wait_ge(b_part3, t - 1)
                    if t0 >= 3:
                        pe.wait_ge(b_sum_ready, t - 2)
                    for i in range(TILES):
                        for j in range(TILES):
                            for part in range(3):
                                last = pe.matmul(bank[6][:, i * F:(i + 1) * F], b_same[s][:, j, i * P:(i + 1) * P],
                                                 b_rows[s][:, part, j * F:(j + 1) * F],
                                                 start=(j == 0 and part == 0), stop=(j == TILES - 1 and part == 2))
                    last.then_inc(b_summed, 1)
                if front:
                    pe.wait_ge(b_s1_ready, t + 1)
                    if t0 >= 1:
                        pe.wait_ge(b_t_ready, t)
                    pe.matmul(bank[4][:, :], wf2[:, :], b_s1[:, :], start=True, stop=True).then_inc(b_filter, 1)

            for u in range(4):
                step_b(0, u, u, mid=u >= 1, back=u >= 2)
            with pe.Fori(2, HALF) as k:
                for u in range(2):
                    step_b(k, u, 4 + u)
            step_b(HALF, 0, 4, front=False)
            step_b(HALF, 1, 5, front=False, mid=False)

            def f_turn(c, q, slot, m, c0):
                if q == 0:
                    pe.wait_ge(f_sum_ld[slot % RN], 16 * (RX // RN * m + slot // RN + 1))
                if c0 >= 2:
                    pe.wait_ge(f_copied, c - 1)
                turn_tiles(bank[q % 2], d_n[slot % RN][:, q * 512:(q + 1) * 512]).then_inc(f_turned, 1)

            def f_first(c, q, c0):
                pe.wait_ge(f_copied, c + 1)
                if c0 >= 2:
                    pe.wait_ge(f_s, c - 1)
                to = bank[2 + q % 2]
                pe.matmul(to[:, :], wo1[:, :], turned[q % 2][:, :], start=True, stop=True).then_inc(f_z, 1)

            def f_second(c, q, c0):
                if c0 >= 2:
                    pe.wait_ge(f_out, c - 1)
                to = bank[4 + q % 2]
                pe.matmul(to[:, :], ones3[:, 0:P], bo23[:, :, :].rearrange("k j f -> k (j f)"), start=True, stop=False)
                pe.wait_ge(f_s, c + 1)
                for j in range(TILES):
                    last = pe.matmul(to[:, j * F:(j + 1) * F], f_ssp_out[q % 2][:, j * P:(j + 1) * P], wo2[:, :],
                                     start=False, stop=(j == TILES - 1))
                last.then_inc(f_y, 1)

            def f_group(g, slot, m, g0):
                for q in range(QUADS):
                    c, c0 = QUADS * g + q, QUADS * g0 + q
                    f_turn(c, q, slot, m, c0)
                    if c0 >= 1:
                        f_first(c - 1, q - 1, c0 - 1)
                    if c0 >= 3:
                        f_second(c - 3, q - 3, c0 - 3)

            for g in range(RX):
                f_group(g, g, 0, g)
            with pe.Fori(1, 1 + ROUNDS) as m:
                for i in range(RX):
                    f_group(m * RX + i, i, m, RX)
            for g in range((1 + ROUNDS) * RX, NG):
                f_group(g, g % RX, g // RX, g)
            c = QUADS * NG
            f_first(c - 1, QUADS - 1, c - 1)
            for n in (3, 2, 1):
                f_second(c - n, QUADS - n, c - n)


_INS = ['x', 'src', 'dst', 'edge_attr_20', 'edge_weight', 'L0_gnn_W_l', 'L0_gnn_b_l', 'L0_gnn_W_r', 'L0_gnn_b_r',
        'L0_gnn_att', 'L0_gnn_bias', 'L1_gnn_W_in2f', 'L1_gnn_Wf1', 'L1_gnn_bf1', 'L1_gnn_Wf2', 'L1_gnn_bf2',
        'L1_gnn_Wo1', 'L1_gnn_bo1', 'L1_gnn_Wo2', 'L1_gnn_bo2']


def kernel(**inputs):
    import numpy as _np
    import concourse.bacc as _bacc
    from concourse import mybir as _mybir
    from concourse.bass_utils import run_bass_kernel_spmd as _run

    nc = _bacc.Bacc("TRN2", target_bir_lowering=False, num_devices=1)
    arrays, args = {}, []
    for name in _INS:
        a = _np.ascontiguousarray(inputs[name])
        arrays[f"in_{name}"] = a
        args.append(nc.dram_tensor(f"in_{name}", a.shape, _mybir.dt.from_np(a.dtype), kind="ExternalInput").ap())
    out = nc.dram_tensor("out", inputs['x'].shape, _mybir.dt.float32, kind="ExternalOutput").ap()
    gnn(nc, *args, out)
    r = _run(nc, [arrays], core_ids=[0])
    return r.results[0]["out"]
```
